# Optimizing a Trainium2 kernel written in Bass

```python
import numpy as np
import jax
import jax.numpy as jnp

def _softmax(x, axis=-1):
    return jax.nn.softmax(x, axis=axis)

def _gelu(x):
    return jax.nn.gelu(x, approximate=True)

def _silu(x):
    return jax.nn.silu(x)

def _sigmoid(x):
    return jax.nn.sigmoid(x)

def _layernorm(x, axis=-1, eps=1e-05):
    m = jnp.mean(x, axis=axis, keepdims=True)
    v = jnp.var(x, axis=axis, keepdims=True)
    return (x - m) / jnp.sqrt(v + eps)

def _scatter_add(tgt, idx, src, axis=0):
    return tgt.at[idx].add(src)

def _segment_sum(src, seg, n):
    return jax.ops.segment_sum(src, seg, n)
kernel_name = 'mk_gnn_ffn_d1_gnn_r8_7a94a8'

def setup_inputs(seed: int=0):
    np.random.seed(seed)
    _w = jnp.asarray

    def _rec_inputs():
        import jax
        import jax.numpy as jnp
        _gk = jax.random.key(seed)
        x = -0.0003713 + 1 * jax.random.normal(jax.random.fold_in(_gk, 1), (6250, 256), jnp.float32)
        src = jax.random.randint(jax.random.fold_in(_gk, 2), (100000,), 0, 6250, jnp.int32)
        dst = jnp.minimum((6250 * jax.random.uniform(jax.random.fold_in(_gk, 3), (100000,)) ** 2.0).astype(jnp.int32), 49999)
        _o = jnp.argsort(dst, stable=True)
        src = src[_o]
        dst = dst[_o]
        return (x, src, dst)
    x, src, dst = _rec_inputs()

    def _L0_gnn_setup():
        import jax, jax.numpy as jnp
        import numpy as np
        N, E, D_IN, D_OUT = (6250, 200000, 256, 256)
        key = jax.random.key(seed)
        k1, k2, k3, k4, k5, k6 = jax.random.split(key, 6)
        x = jax.random.normal(k1, (N, D_IN), dtype=jnp.float32)
        edge_index = jax.random.randint(k2, (2, E), 0, N, dtype=jnp.int64)
        s = 1.0 / np.sqrt(D_IN)
        W1 = jax.random.uniform(k3, (D_OUT, D_IN), minval=-s, maxval=s, dtype=jnp.float32)
        b1 = jax.random.uniform(k4, (D_OUT,), minval=-s, maxval=s, dtype=jnp.float32)
        W2 = jax.random.uniform(k5, (D_OUT, D_IN), minval=-s, maxval=s, dtype=jnp.float32)
        b2 = jax.random.uniform(k6, (D_OUT,), minval=-s, maxval=s, dtype=jnp.float32)
        return {'x': x, 'W1': W1, 'b1': b1, 'W2': W2, 'b2': b2, 'edge_index': edge_index}
    _L0_gnn_all = _L0_gnn_setup()
    _L0_gnn_in = {k: v for k, v in _L0_gnn_all.items() if k in ('W1', 'b1', 'W2', 'b2')}
    del _L0_gnn_all

    def _L0_ffn_setup():
        import jax, jax.numpy as jnp
        import numpy as np
        B, S, D, H, E, K = (8, 1024, 256, 1024, 8, 2)
        key = jax.random.key(seed)
        ks = jax.random.split(key, 7)
        s_in = 1.0 / np.sqrt(D)
        s_hid = 1.0 / np.sqrt(H)
        return {'x': jax.random.normal(ks[0], (B, S, D), dtype=jnp.float32), 'Wg': jax.random.uniform(ks[1], (E, D), jnp.float32, -s_in, s_in), 'bg': jax.random.uniform(ks[2], (E,), jnp.float32, -s_in, s_in), 'W1': jax.random.uniform(ks[3], (E, H, D), jnp.float32, -s_in, s_in), 'b1': jax.random.uniform(ks[4], (E, H), jnp.float32, -s_in, s_in), 'W2': jax.random.uniform(ks[5], (E, D, H), jnp.float32, -s_hid, s_hid), 'b2': jax.random.uniform(ks[6], (E, D), jnp.float32, -s_hid, s_hid)}
    _L0_ffn_all = _L0_ffn_setup()
    _L0_ffn_in = {k: v for k, v in _L0_ffn_all.items() if k in ('Wg', 'bg', 'W1', 'b1', 'W2', 'b2')}
    del _L0_ffn_all
    return {'x': x, 'src': src, 'dst': dst, 'L0_gnn_W1': _L0_gnn_in['W1'], 'L0_gnn_b1': _L0_gnn_in['b1'], 'L0_gnn_W2': _L0_gnn_in['W2'], 'L0_gnn_b2': _L0_gnn_in['b2'], 'L0_ffn_Wg': _L0_ffn_in['Wg'], 'L0_ffn_bg': _L0_ffn_in['bg'], 'L0_ffn_W1': _L0_ffn_in['W1'], 'L0_ffn_b1': _L0_ffn_in['b1'], 'L0_ffn_W2': _L0_ffn_in['W2'], 'L0_ffn_b2': _L0_ffn_in['b2']}

def reference(x, src, dst, L0_gnn_W1, L0_gnn_b1, L0_gnn_W2, L0_gnn_b2, L0_ffn_Wg, L0_ffn_bg, L0_ffn_W1, L0_ffn_b1, L0_ffn_W2, L0_ffn_b2):
    import jax
    import jax.numpy as jnp

    def _L0_gnn_ref(x, W1, b1, W2, b2, edge_index):
        import jax, jax.numpy as jnp
        import numpy as np
        N, E, D_IN, D_OUT = (6250, 200000, 256, 256)
        dst = edge_index[0]
        nbr = edge_index[1]
        n = x.shape[0]
        agg = jax.ops.segment_sum(x[nbr], dst, num_segments=n)
        cnt = jax.ops.segment_sum(jnp.ones((nbr.shape[0],), x.dtype), dst, num_segments=n)
        mean = agg / jnp.maximum(cnt, 1.0)[:, None]
        return x @ W1.T + b1 + mean @ W2.T + b2

    def _L0_ffn_ref(x, Wg, bg, W1, b1, W2, b2):
        import jax, jax.numpy as jnp
        import numpy as np
        B, S, D, H, E, K = (8, 1024, 256, 1024, 8, 2)
        gate_scores = jnp.einsum('bsd,ed->bse', x, Wg) + bg
        topk_scores, topk_idx = jax.lax.top_k(gate_scores, K)
        topk_probs = jax.nn.softmax(topk_scores, axis=-1)
        combine = jnp.sum(topk_probs[..., None] * jax.nn.one_hot(topk_idx, E, dtype=x.dtype), axis=-2)
        out = jnp.zeros_like(x)
        for e in range(E):
            h = jax.nn.relu(jnp.einsum('bsd,hd->bsh', x, W1[e]) + b1[e])
            y = jnp.einsum('bsh,dh->bsd', h, W2[e]) + b2[e]
            out = out + combine[..., e:e + 1] * y
        return out
    edge_index = jnp.stack([src, dst])
    x = x + _L0_gnn_ref(_layernorm(x, axis=-1), L0_gnn_W1, L0_gnn_b1, L0_gnn_W2, L0_gnn_b2, edge_index)
    x = x + _L0_ffn_ref(_layernorm(x, axis=-1)[None], L0_ffn_Wg, L0_ffn_bg, L0_ffn_W1, L0_ffn_b1, L0_ffn_W2, L0_ffn_b2)[0]
    return x

_drawn_inputs = setup_inputs


def setup_inputs(seed=0):
    import zlib

    import numpy as np

    out = dict(_drawn_inputs(seed))
    spreads = {}
    factors = {'L0_ffn_b1': 6.405, 'L0_ffn_b2': 5.036}
    for name, (base, spread) in spreads.items():
        noise = np.random.default_rng([zlib.crc32(name.encode()), seed]).standard_normal(out[name].shape)
        drawn = base * np.exp(spread * noise) if base else spread * noise
        out[name] = jnp.asarray(drawn.astype(out[name].dtype))
    for name, factor in factors.items():
        out[name] = (out[name] * factor).astype(out[name].dtype)
    return out
```

```python
from contextlib import ExitStack

import concourse.bass as bass
from concourse import mybir

ALU = mybir.AluOpType
ACT = mybir.ActivationFunctionType
AX = mybir.AxisListType
F32 = mybir.dt.float32
F16 = mybir.dt.float16
I32 = mybir.dt.int32
U16 = mybir.dt.uint16
ENG = mybir.EngineType

P = 128
N = 6250
D = 256
DK = D // P
H = 1024
HB = H // P
E = 8
K = 2
EDGES = 100000
NT = -(-N // P)
TAIL = N - (NT - 1) * P
U = 7
NB = NT // U
NP = NT * P
W = D + 1
EPS = 1e-5

EP = 125
EC = EDGES // EP
COLS = [144, 328, 328]


def most_blocks(n, buckets, size):
    return (n + buckets * (size - 1)) // size


R = 16
CH = [-(-most_blocks(EP * c, NT, P) // R) * R for c in COLS]
CH0 = [sum(CH[:g]) for g in range(len(CH))]
NCH = sum(CH)
CMAX, CHMAX = max(COLS), max(CH)
PU = 8
LOOK = 2
NPS = 4

T = 256
TT = T // P
TILES = most_blocks(K * N, E, T)
TILES += TILES % 2
SLOTS = TILES * T
SC = SLOTS // P
RU = 14
RING = [4] * len(COLS) + [2]


class Count:

    def __init__(self):
        self.at = 0
        self.k = 0

    def enter(self, i, per):
        self.before, self.per = self.at + self.k, per
        self.at, self.k = self.before + i * per, 0

    def leave(self, trips):
        assert self.k == self.per
        self.at, self.k = self.before + trips * self.per, 0

    def value(self):
        return self.at + self.k

    def up(self):
        self.k += 1
        return self.value()


def gnn_moe(nc, x, src, dst, gw1t, gw2t, gb1, gb2, wgt, bg, w1, b1, w2, b2, out):
    ytab = nc.dram_tensor("ytab", [NP, D], F32, kind="Internal").ap()
    xtab = nc.dram_tensor("xtab", [NP, D], F32, kind="Internal").ap()
    ztab = nc.dram_tensor("ztab", [K * N + SLOTS, D], F32, kind="Internal").ap()

    with ExitStack() as ctx:
        def sb(name, shape, dt=F32):
            return ctx.enter_context(nc.sbuf_tensor(name, shape, dt))

        def sem(name):
            return ctx.enter_context(nc.semaphore(name))

        bank = [ctx.enter_context(nc.psum_tensor(f"bank{i}", [P, 512], F32)) for i in range(8)]

        ident = sb("ident", [P, P])
        ones = sb("ones", [P, P])
        before = sb("before", [P, P])
        iota = sb("iota", [P, P])
        iota_q = sb("iota_q", [P, P], F16)
        iota_c = sb("iota_c", [P, CHMAX], F16)
        zero16 = sb("zero16", [P, P], F16)
        earlier = sb("earlier", [P, E, E])
        part = sb("part", [P, 1])
        node = sb("node", [P, NT, D])
        agg = sb("agg", [P, NT * W])
        agg3 = agg[:, :].rearrange("p (t w) -> p t w", w=W)
        xn = sb("xn", [P, U, D])
        xnT = sb("xnT", [P, U, D])
        yout = sb("yout", [P, U, D])
        stats = sb("stats", [P, U, 6])
        mv = sb("mv", [P, NT, 2])
        mvt = sb("mvt", [P, U, 2])
        std = sb("std", [P, NT])
        rstd = sb("rstd", [P, NT])
        eps = sb("eps", [P, 1])
        rcnt = sb("rcnt", [P, NT])
        gw = sb("gw", [P, 2, DK, D])
        gb = sb("gb", [P, 2, D])
        gate_w = sb("gate_w", [P, DK, E])
        gate_b = sb("gate_b", [P, E])
        rowidx = sb("rowidx", [P, NCH], I32)
        local = sb("local", [P, NCH + LOOK])
        offs = sb("offs", [1, NCH], I32)
        stage = sb("stage", [P, R], I32)
        onehot = sb("onehot", [P, NPS, P])
        tot = sb("tot", [P, NT])
        nbuck = sb("nbuck", [P, 4])
        nbuck_i = sb("nbuck_i", [P, 2], I32)
        diag = sb("diag", [P, NT])
        base = sb("base", [P, NT])
        ge = sb("ge", [P, CHMAX])
        ohq = sb("ohq", [P, 4, P], F16)
        ohc = sb("ohc", [P, 4, CHMAX], F16)
        val = sb("val", [P, 4, 2, P], F16)
        got = sb("got", [P, 6, CHMAX], I32)
        prob = sb("prob", [P, K, NT])
        gidx = sb("gidx", [P, SC], I32)
        sidx = sb("sidx", [P, SC], I32)
        texp = sb("texp", [1, TILES], I32)
        gstage = sb("gstage", [P, 2, TT], I32)
        sstage = sb("sstage", [P, 2, TT], I32)

        arena = sb("arena", [P, 10752])
        room = [0]

        def take(n, dt=F32):
            a = room[0]
            room[0] += n
            assert room[0] <= 10752
            v = arena[:, a:a + n]
            return v if dt is F32 else v.bitcast(dt)

        rows = take(R * W).rearrange("p (r w) -> p r w", w=W)
        src_i, dst_i = take(EC, I32), take(EC, I32)
        blk16 = take(EC // 2, F16)
        val1, val2 = take(EC), take(EC)
        pos, pos_c, pos_q = take(CMAX), take(CMAX), take(CMAX)
        tmp_i = take(EC, I32)
        inb = take(U * CMAX // 2, U16).rearrange("p (u c) -> p u c", u=U)

        room[0] = 0
        score = take(NT * E).rearrange("p (t e) -> p t e", e=E)
        pair = [take(NT * E * E).rearrange("p (t e f) -> p t e f", e=E, f=E) for _ in range(2)]
        rank = take(NT * E).rearrange("p (t e) -> p t e", e=E)
        sel = [take(NT * E).rearrange("p (t e) -> p t e", e=E) for _ in range(3)]
        cum = take(E * NT).rearrange("p (e t) -> p e t", t=NT)
        prod = take(NT * E).rearrange("p (t e) -> p t e", e=E)
        top = take(K * NT).rearrange("p (k t) -> p k t", k=K)
        ex = take(NT)
        tokpos = take(NT * K).rearrange("p (t k) -> p t k", k=K)
        tok_i = [take(NT * K, I32) for _ in range(3)]
        tok_c, tok_q, tok_v1, tok_v2 = (take(NT * K) for _ in range(4))
        slotid = take(SC)
        vcol = take(2)

        room[0] = 0
        w1b = take(2 * DK * H).rearrange("p (b k h) -> p b k h", b=2, k=DK)
        w2b = take(2 * HB * D).rearrange("p (b k d) -> p b k d", b=2, k=HB)
        hT = take(2 * HB * T // 2 * 1).rearrange("p (k n) -> p k n", k=HB)
        b1b = sb("b1b", [P, 2, HB])
        b2b = sb("b2b", [P, 2, D])
        xg = xn[:, 0:4, :].rearrange("p (b n) d -> p b n d", b=2)
        xgT = xnT[:, 0:4, :].rearrange("p (b k) n -> p b k n", b=2)
        ysb = yout[:, 0:4, :].rearrange("p (b n) d -> p b n d", b=2)
        z = [w1b.rearrange("p b k h -> p b (k h)")[:, :, 0:U * D].rearrange("p b (u d) -> p b u d", d=D),
             w2b.rearrange("p b k d -> p b (k d)")[:, :, 0:U * D].rearrange("p b (u d) -> p b u d", d=D)]

        G = range(len(COLS))
        s_const, s_tail0, s_x, s_edge, s_w = (sem(n) for n in ("consts", "tail_zeroed", "x_in", "edges_in", "weights_in"))
        s_prep = sem("values_ready")
        s_tot = [sem(f"totals{g}") for g in G] + [sem("totals_e")]
        s_nb = [sem(f"counted{g}") for g in G] + [sem("counted_e")]
        s_nch = [sem(f"rounded{g}") for g in G] + [sem("rounded_e")]
        s_sc = [sem(f"starts{g}") for g in G] + [sem("starts_e")]
        s_dg = [sem(f"spread{g}") for g in G] + [sem("spread_e")]
        s_bs = [sem(f"bases{g}") for g in G] + [sem("bases_e")]
        s_qc = [sem(f"onehots{g}") for g in G] + [sem("onehots_e")]
        s_val = [sem(f"scaled{g}") for g in G] + [sem("scaled_e")]
        s_pl = [sem(f"placed{g}") for g in G] + [sem("placed_e")]
        s_tab = sem("tables_ready")
        s_mv, s_std, s_rs = sem("moments"), sem("std"), sem("rstd")
        s_xn, s_tr, s_xT = sem("normed"), sem("transposed"), sem("xT_ready")
        s_mm, s_bias, s_add, s_y, s_yst = (sem(n) for n in ("linear_done", "biased", "self_added", "y_copied", "y_stored"))
        s_v = sem("vector_steps")
        s_stage, s_oh, s_agg, s_sum = sem("staged"), sem("onehot_ready"), sem("chunk_multiplied"), sem("chunk_summed")
        s_row = [sem(f"rows_in{r}") for r in range(R)]
        s_mv2, s_std2, s_xn2, s_tr2, s_xT2 = (sem(n) for n in ("moments2", "std2", "normed2", "transposed2", "xT2_ready"))
        s_gate, s_gadd, s_xst = sem("gates_done"), sem("gates_read"), sem("xtab_stored")
        s_dif, s_exp = sem("difference"), sem("exp_done")
        s_route = sem("routed")
        s_pass = sem("passed")
        s_gst, s_sst = sem("gather_staged"), sem("scatter_staged")
        s_g2, s_sc2 = [sem(f"tokens_in{b}") for b in (0, 1)], [sem(f"tokens_out{b}") for b in (0, 1)]
        s_w1, s_w2 = [sem(f"w1_in{b}") for b in (0, 1)], [sem(f"w2_in{b}") for b in (0, 1)]
        s_ft, s_fx, s_fh, s_fr, s_fy, s_fo = (sem(n) for n in (
            "ffn_transposed", "ffn_xT", "ffn_hidden", "ffn_relu", "ffn_out", "ffn_biased"))
        s_z, s_mix, s_out = [sem("z_in0"), sem("z_in1")], sem("mixed"), sem("out_stored")

        x_v = x[0:(NT - 1) * P, :].rearrange("(t p) d -> p t d", p=P)
        y_v = ytab.rearrange("(i u p) d -> i p u d", u=U, p=P)
        xt_v = xtab.rearrange("(i u p) d -> i p u d", u=U, p=P)

        block = ctx.enter_context(nc.Block())

        @block.sync
        def _(sp):
            sp.dma_start(src_i[0:EP, :], src.rearrange("(p c) -> p c", p=EP)).then_inc(s_edge, 16)
            sp.dma_start(dst_i[0:EP, :], dst.rearrange("(p c) -> p c", p=EP)).then_inc(s_edge, 16)
            for a in range(0, NT - 1, 12):
                sp.dma_start(node[:, a:a + 12, :], x_v[:, a:a + 12, :]).then_inc(s_x, 16)
            sp.wait_ge(s_tail0, 1)
            sp.dma_start(node[0:TAIL, NT - 1, :], x[(NT - 1) * P:N, :]).then_inc(s_x, 16)
            sp.dma_start(gw[:, 0], gw1t.rearrange("(k p) n -> p k n", p=P)).then_inc(s_w, 16)
            sp.dma_start(gw[:, 1], gw2t.rearrange("(k p) n -> p k n", p=P)).then_inc(s_w, 16)
            sp.dma_start(gb[:, 0], gb1.rearrange("(a n) -> a n", a=1).to_broadcast([P, D])).then_inc(s_w, 16)
            sp.dma_start(gb[:, 1], gb2.rearrange("(a n) -> a n", a=1).to_broadcast([P, D])).then_inc(s_w, 16)
            sp.dma_start(gate_w[:, :, :], wgt.rearrange("p (k e) -> p k e", e=E)).then_inc(s_w, 16)
            sp.dma_start(gate_b[:, :], bg.rearrange("(a n) -> a n", a=1).to_broadcast([P, E])).then_inc(s_w, 16)
            with sp.Fori(0, NB) as i:
                sp.wait_ge(s_y, i * U + U)
                sp.dma_start(y_v[bass.ds(i, 1)].rearrange("i p u d -> p (i u) d"), yout[:, :, :]).then_inc(s_yst, 16)
            with sp.Fori(0, NB) as i:
                sp.wait_ge(s_xn2, i * U + U)
                sp.dma_start(xt_v[bass.ds(i, 1)].rearrange("i p u d -> p (i u) d"), xn[:, :, :]).then_inc(s_xst, 16)
            sp.wait_ge(s_route, 1)

            def weights(j, b, first):
                e = sp.value_load(texp[0:1, bass.ds(j, 1)], min_val=0, max_val=E - 1)
                if not first:
                    sp.wait_ge(s_fh, (j - 1) * HB)
                    sp.wait_ge(s_fr, (j - 1) * HB)
                sp.dma_start(w1b[:, b].rearrange("p k h -> p (k h)"),
                             w1[bass.ds(e, 1)].rearrange("e p n -> (e p) n")).then_inc(s_w1[b], 16)
                sp.dma_start(b1b[:, b], b1[bass.ds(e, 1)].rearrange("e p n -> (e p) n")).then_inc(s_w1[b], 16)
                if not first:
                    sp.wait_ge(s_fo, j - 1)
                sp.dma_start(w2b[:, b].rearrange("p k d -> p (k d)"),
                             w2[bass.ds(e, 1)].rearrange("e p n -> (e p) n")).then_inc(s_w2[b], 16)
                sp.dma_start(b2b[:, b], b2[bass.ds(e, 1), :].to_broadcast([P, D])).then_inc(s_w2[b], 16)

            for j in range(2):
                weights(j, j, True)
            with sp.Fori(1, TILES // 2) as i:
                for b in range(2):
                    weights(i * 2 + b, b, False)
            for b in range(2):
                sp.wait_ge(s_sc2[b], 16 * TT * TILES // 2)
            sp.wait_ge(s_fo, TILES)
            for i in range(NB):
                b = i % 2
                if i >= 2:
                    sp.wait_ge(s_mix, (i - 1) * U)
                for k in range(K):
                    a = k * N + i * U * P
                    full = U if i < NB - 1 else U - 1
                    sp.dma_start(z[k][:, b, 0:full], ztab[a:a + full * P, :].rearrange("(u p) d -> p u d", p=P)).then_inc(s_z[b], 16)
                    if full < U:
                        a += full * P
                        sp.dma_start(z[k][0:TAIL, b, full], ztab[a:a + TAIL, :]).then_inc(s_z[b], 16)
            for i in range(NB):
                sp.wait_ge(s_mix, (i + 1) * U)
                full = U if i < NB - 1 else U - 1
                a = i * U * P
                sp.dma_start(out[a:a + full * P, :].rearrange("(u p) d -> p u d", p=P), node[:, i * U:i * U + full, :]).then_inc(s_out, 16)
                if full < U:
                    a += full * P
                    sp.dma_start(out[a:N, :], node[0:TAIL, NT - 1, :]).then_inc(s_out, 16)
            sp.wait_ge(s_out, 16 * (NB + 1))

        @block.gpsimd
        def _(pool):
            pool.memset(node[:, NT - 1, :], 0.0).then_inc(s_tail0, 1)
            pool.memset(ones[:, :], 1.0).then_inc(s_const, 1)
            pool.iota(iota[:, :], pattern=[[1, P]], base=0, channel_multiplier=0, allow_small_or_imprecise_dtypes=True).then_inc(s_const, 1)
            pool.iota(iota_q[:, :], pattern=[[1, P]], base=0, channel_multiplier=0, allow_small_or_imprecise_dtypes=True).then_inc(s_const, 1)
            pool.iota(iota_c[:, :], pattern=[[1, CHMAX]], base=0, channel_multiplier=0, allow_small_or_imprecise_dtypes=True).then_inc(s_const, 1)
            pool.iota(part[:, :], pattern=[[1, 1]], base=0, channel_multiplier=1, allow_small_or_imprecise_dtypes=True).then_inc(s_const, 1)
            pool.memset(zero16[:, :], 0.0).then_inc(s_const, 1)
            pool.memset(eps[:, :], EPS).then_inc(s_const, 1)
            pool.wait_ge(s_const, 7)
            pool.affine_select(out=ident[:, :], in_=ones[:, :], compare_op=ALU.is_equal, fill=0.0, base=0,
                               pattern=[[-1, P]], channel_multiplier=1).then_inc(s_const, 1)
            pool.affine_select(out=before[:, :], in_=ones[:, :], compare_op=ALU.is_gt, fill=0.0, base=0,
                               pattern=[[1, P]], channel_multiplier=-1).then_inc(s_const, 1)
            pool.affine_select(out=earlier[:, :, :], in_=ones[:, 0:E * E].rearrange("p (e f) -> p e f", e=E),
                               compare_op=ALU.is_gt, fill=0.0, base=0,
                               pattern=[[1, E], [-1, E]], channel_multiplier=0).then_inc(s_const, 1)
            pool.memset(agg[:, :], 0.0).then_inc(s_const, 1)
            pool.memset(rows[:, :, D:W], 1.0).then_inc(s_const, 1)
            pool.memset(local[:, NCH:NCH + LOOK], 0.0).then_inc(s_const, 1)
            pool.wait_ge(s_w, 16 * 6)
            pool.tensor_tensor(gb[:, 0], gb[:, 0], gb[:, 1], ALU.add).then_inc(s_const, 1)
            pool.wait_ge(s_const, 14)
            with pool.Fori(0, NB) as i:
                pool.wait_ge(s_xn, i * U + U)
                pool.tensor_tensor(node[:, bass.ds(i * U, U), :], node[:, bass.ds(i * U, U), :],
                                   gb[:, 0:1, :].to_broadcast([P, U, D]), ALU.add).then_inc(s_bias, 1)

            pool.wait_ge(s_yst, 16 * NB)

            def gathers(i, first):
                for r in range(R):
                    if r % (R // 2) == 0:
                        pool.wait_ge(s_stage, i * 2 + r // (R // 2) + 1)
                    if not first:
                        pool.wait_ge(s_agg, (i - 1) * R + r + 1)
                        pool.sem_inc(s_pass)
                    pool.indirect_dma_start(out=rows[:, r, 0:D], out_offset=None, in_=ytab[:, :],
                                            in_offset=bass.IndirectOffsetOnAxis(ap=stage[:, r:r + 1], axis=0)).then_inc(s_row[r], 16)

            gathers(0, True)
            with pool.Fori(1, NCH // R) as i:
                gathers(i, False)

            pool.wait_ge(s_xst, 16 * NB)
            pool.wait_ge(s_tr2, NT)

            def fetch(j, b, wait):
                pool.wait_ge(s_gst, j + 1)
                if wait:
                    pool.wait_ge(s_ft, j - 1)
                pool.sem_inc(s_pass)
                for n in range(TT):
                    pool.indirect_dma_start(out=xg[:, b, n, :], out_offset=None, in_=xtab[:, :],
                                            in_offset=bass.IndirectOffsetOnAxis(ap=gstage[:, b, n:n + 1], axis=0)).then_inc(s_g2[b], 16)

            def deliver(j, b):
                pool.wait_ge(s_sst, j + 1)
                pool.wait_ge(s_fo, j + 1)
                pool.sem_inc(s_pass)
                for n in range(TT):
                    pool.indirect_dma_start(out=ztab[:, :], out_offset=bass.IndirectOffsetOnAxis(ap=sstage[:, b, n:n + 1], axis=0),
                                            in_=ysb[:, b, n, :], in_offset=None).then_inc(s_sc2[b], 16)

            fetch(0, 0, False)
            fetch(1, 1, False)
            with pool.Fori(0, TILES // 2 - 1) as i:
                for b in range(2):
                    deliver(i * 2 + b, b)
                    fetch(i * 2 + b + 2, b, True)
            for b in range(2):
                deliver(TILES - 2 + b, b)

        @block.scalar
        def _(act):
            act.wait_ge(s_const, 7)
            act.wait_ge(s_mv, NB)
            act.activation(std[:, :], mv[:, :, 1], ACT.Sqrt, bias=eps[:, 0:1]).then_inc(s_std, 1)
            def linear_out(i, first):
                for u in range(U + 1):
                    if u < U:
                        act.wait_ge(s_tr, i * U + u + 1)
                        act.activation(xnT[:, u, :], bank[u % 2][:, 0:D], ACT.Copy).then_inc(s_xT, 1)
                    if u > 0:
                        act.wait_ge(s_mm, i * U + u)
                        if u == 1 and not first:
                            act.wait_ge(s_yst, i * 16)
                        act.activation(yout[:, u - 1, :], bank[4 + (u - 1) % 2][:, 0:D], ACT.Copy).then_inc(s_y, 1)

            linear_out(0, True)
            with act.Fori(1, NB) as i:
                linear_out(i, False)

            def scaled(g, c, w, lanes, v1, v2):
                act.wait_ge(s_qc[g], 2 * c + 1)
                if w is not None:
                    act.wait_ge(s_pl[g], w)
                act.activation(val[0:lanes, w_slot[0], 0, :], ohq[0:lanes, w_slot[0], :], ACT.Copy, scale=v1)
                act.activation(val[0:lanes, w_slot[0], 1, :], ohq[0:lanes, w_slot[0], :], ACT.Copy, scale=v2).then_inc(s_val[g], 1)

            w_slot = [0]

            def scale_columns(g, lanes, trips, unroll, v1, v2, c0):
                for u in range(unroll):
                    w_slot[0] = u % RING[g]
                    scaled(g, u, None if u < RING[g] else u - RING[g] + 1, lanes, v1[0:lanes, c0 + u:c0 + u + 1], v2[0:lanes, c0 + u:c0 + u + 1])
                with act.Fori(1, trips) as i:
                    for u in range(unroll):
                        w_slot[0] = u % RING[g]
                        scaled(g, i * unroll + u, i * unroll + u - RING[g] + 1, lanes,
                               v1[0:lanes, bass.ds(i * unroll + u + c0, 1)], v2[0:lanes, bass.ds(i * unroll + u + c0, 1)])

            for g in G:
                scale_columns(g, EP, COLS[g] // PU, PU, val1, val2, sum(COLS[:g]))
            act.wait_ge(s_tab, len(COLS))

            def staging(i, first):
                for h in range(2):
                    if not first:
                        act.wait_ge(s_agg, (i - 1) * R + (h + 1) * (R // 2))
                    act.activation(stage[:, h * (R // 2):(h + 1) * (R // 2)], rowidx[:, bass.ds(i * R + h * (R // 2), R // 2)],
                                   ACT.Copy).then_inc(s_stage, 1)

            staging(0, True)
            with act.Fori(1, NCH // R) as i:
                staging(i, False)

            act.wait_ge(s_mv2, NB)
            act.activation(std[:, :], mv[:, :, 1], ACT.Sqrt, bias=eps[:, 0:1]).then_inc(s_std2, 1)
            with act.Fori(0, NB) as i:
                for u in range(U):
                    act.wait_ge(s_tr2, i * U + u + 1)
                    act.activation(xnT[:, u, :], bank[u % 2][:, 0:D], ACT.Copy).then_inc(s_xT2, 1)
            act.wait_ge(s_dif, 1)
            act.activation(ex[:, :], top[:, 1], ACT.Exp).then_inc(s_exp, 1)
            scale_columns(len(COLS), P, NT * K // RU, RU, tok_v1, tok_v2, 0)

            act.wait_ge(s_route, 1)

            def gstaging(j, b, wait):
                if wait:
                    act.wait_ge(s_ft, j - 1)
                act.activation(gstage[:, b], gidx[:, bass.ds(j * TT, TT)], ACT.Copy).then_inc(s_gst, 1)

            def relu(j, b, first):
                if first:
                    act.activation(sstage[:, b], sidx[:, j * TT:(j + 1) * TT], ACT.Copy).then_inc(s_sst, 1)
                else:
                    act.wait_ge(s_sc2[b], (i_half[0]) * 16 * TT)
                    act.activation(sstage[:, b], sidx[:, bass.ds(j * TT, TT)], ACT.Copy).then_inc(s_sst, 1)
                act.wait_ge(s_w1[b], (i_half[0] + 1) * 32)
                for m in range(HB):
                    act.wait_ge(s_fh, j * HB + m + 1)
                    if not (first and j == 0) and m == 0:
                        act.wait_ge(s_fy, j)
                    act.activation(hT[:, m, :], bank[1 + m % 4][:, 0:T], ACT.Relu, bias=b1b[:, b, m:m + 1]).then_inc(s_fr, 1)

            i_half = [0]
            for j in range(2):
                gstaging(j, j, False)
            for j in range(2):
                relu(j, j, True)
                gstaging(j + 2, j, True)
            with act.Fori(1, TILES // 2 - 1) as i:
                i_half[0] = i
                for b in range(2):
                    relu(i * 2 + b, b, False)
                    gstaging(i * 2 + b + 2, b, True)
            i_half[0] = TILES // 2 - 1
            for b in range(2):
                relu(TILES - 2 + b, b, False)

        @block.tensor
        def _(pe):
            pe.wait_ge(s_const, 14)

            def transposes(i, u, s_in, s_done, s_free):
                pe.wait_ge(s_in, i * U + u + 1)
                back = 1 if u == 0 else 3 if u == 1 else 2
                if not (isinstance(i, int) and u < 2):
                    pe.wait_ge(s_free, i * U + u - back + 1)
                for k in range(DK):
                    mm = pe.transpose(bank[u % 2][:, k * P:(k + 1) * P], xn[:, u, k * P:(k + 1) * P], ident[:, :])
                mm.then_inc(s_done, 1)

            def bucket_sums(g, lanes, nb):
                pe.wait_ge(s_tot[g], NB if g < len(CH) else 1)
                pe.matmul(bank[6][0:nb, 0:1], tot[0:lanes, 0:nb], ones[0:lanes, 0:1], start=True, stop=True).then_inc(s_nb[g], 1)
                pe.wait_ge(s_nch[g], 1)
                pe.matmul(bank[6][0:nb, 0:1], before[0:nb, 0:nb], nbuck[0:nb, 1:2], start=True, stop=True).then_inc(s_sc[g], 1)
                pe.wait_ge(s_dg[g], 1)
                pe.matmul(bank[6][0:lanes, 0:nb], before[0:lanes, 0:lanes], tot[0:lanes, 0:nb], start=True, stop=False)
                pe.matmul(bank[6][0:lanes, 0:nb], ones[0:nb, 0:lanes], diag[0:nb, 0:nb], start=False, stop=True)
                n = CH[g] if g < len(CH) else TILES
                pe.matmul(bank[7][0:1, 0:n], ones[0:nb, 0:1], ge[0:nb, 0:n], start=True, stop=True).then_inc(s_bs[g], 1)

            def place(g, lanes, trips, unroll, n):
                for v in range(2):
                    pe.matmul(bank[4 + v][:, 0:n], zero16[0:lanes, :], iota_c[0:lanes, 0:n], start=True, stop=False)
                with pe.Fori(0, trips) as i:
                    for u in range(unroll):
                        c = i * unroll + u
                        pe.wait_ge(s_qc[g], 2 * c + 2)
                        pe.wait_ge(s_val[g], c + 1)
                        for v in range(2):
                            mm = pe.matmul(bank[4 + v][:, 0:n], val[0:lanes, u % RING[g], v, :], ohc[0:lanes, u % RING[g], 0:n], start=False, stop=False)
                        mm.then_inc(s_pl[g], 1)
                for v in range(2):
                    mm = pe.matmul(bank[4 + v][:, 0:n], zero16[0:lanes, :], iota_c[0:lanes, 0:n], start=False, stop=True)
                mm.then_inc(s_pl[g], 1)

            bucket_sums(0, EP, NT)
            def linear(i):
                for u in range(U + 1):
                    if u < U:
                        transposes(i, u, s_xn, s_tr, s_xT)
                    if u > 0:
                        m = u - 1
                        pe.wait_ge(s_xT, i * U + m + 1)
                        back = 1 if m == 0 else 3 if m == 1 else 2
                        if not (isinstance(i, int) and m < 2):
                            pe.wait_ge(s_y, i * U + m - back + 1)
                            pe.wait_ge(s_add, i * U + m - back + 1)
                        for half in range(2):
                            for k in range(DK):
                                mm = pe.matmul(bank[2 + 2 * half + m % 2][:, 0:D], xnT[:, m, k * P:(k + 1) * P], gw[:, half, k, :],
                                               start=(k == 0), stop=(k == DK - 1))
                        mm.then_inc(s_mm, 1)

            linear(0)
            with pe.Fori(1, NB) as i:
                linear(i)
            pe.wait_ge(s_y, NT)
            for g in G:
                if g:
                    bucket_sums(g, EP, NT)
                place(g, EP, COLS[g] // PU, PU, CH[g])

            def multiply(i, first):
                for r in range(R):
                    n = i * R + r
                    pe.wait_ge(s_row[r], i * 16 + 16)
                    pe.wait_ge(s_oh, n + 1)
                    if not (first and r < NPS):
                        pe.wait_ge(s_sum, n - NPS + 1)
                    pe.matmul(bank[r % NPS][:, 0:W], onehot[:, r % NPS, :], rows[:, r, :], start=True, stop=True).then_inc(s_agg, 1)

            pe.wait_ge(s_add, NT)
            multiply(0, True)
            with pe.Fori(1, NCH // R) as i:
                multiply(i, False)
            pe.wait_ge(s_sum, NCH)

            def gates(i):
                for u in range(U + 1):
                    if u < U:
                        transposes(i, u, s_xn2, s_tr2, s_xT2)
                    if u > 0:
                        m = u - 1
                        pe.wait_ge(s_xT2, i * U + m + 1)
                        if m == 0 and not isinstance(i, int):
                            pe.wait_ge(s_gadd, i)
                        for k in range(DK):
                            mm = pe.matmul(bank[2][:, m * E:(m + 1) * E], xnT[:, m, k * P:(k + 1) * P], gate_w[:, k, :],
                                           start=(k == 0), stop=(k == DK - 1))
                        mm.then_inc(s_gate, 1)

            gates(0)
            with pe.Fori(1, NB) as i:
                gates(i)
            bucket_sums(len(COLS), P, E)
            place(len(COLS), P, NT * K // RU, RU, SC)

            def turn(j, b, half, first):
                pe.wait_ge(s_g2[b], (half + 1) * 16 * TT)
                if not first:
                    pe.wait_ge(s_fx, j)
                for k in range(DK):
                    for n in range(TT):
                        mm = pe.transpose(bank[0][:, k * T + n * P:k * T + (n + 1) * P], xg[:, b, n, k * P:(k + 1) * P], ident[:, :])
                mm.then_inc(s_ft, 1)

            def hidden(j, b, half):
                pe.wait_ge(s_fx, j + 1)
                pe.wait_ge(s_w1[b], (half + 1) * 32)
                for m in range(HB):
                    if not (isinstance(j, int) and j == 0 and m < 4):
                        pe.wait_ge(s_fr, j * HB + m - 3)
                    for k in range(DK):
                        mm = pe.matmul(bank[1 + m % 4][:, 0:T], w1b[:, b, k, m * P:(m + 1) * P], xgT[:, b, k, :],
                                       start=(k == 0), stop=(k == DK - 1))
                    mm.then_inc(s_fh, 1)

            def output(j, b, half, first):
                pe.wait_ge(s_w2[b], (half + 1) * 32)
                if not first:
                    pe.wait_ge(s_fo, j - 1)
                for n in range(TT):
                    for m in range(HB):
                        if n == 0:
                            pe.wait_ge(s_fr, j * HB + m + 1)
                        mm = pe.matmul(bank[5 + b][:, n * D:(n + 1) * D], hT[:, m, n * P:(n + 1) * P], w2b[:, b, m, :],
                                       start=(m == 0), stop=(m == HB - 1))
                mm.then_inc(s_fy, 1)

            pe.wait_ge(s_route, 1)
            turn(0, 0, 0, True)
            hidden(0, 0, 0)
            turn(1, 1, 0, False)
            output(0, 0, 0, True)
            hidden(1, 1, 0)
            turn(2, 0, 1, False)
            output(1, 1, 0, True)
            with pe.Fori(1, TILES // 2 - 1) as i:
                for b in range(2):
                    hidden(i * 2 + b, b, i)
                    turn(i * 2 + b + 1, 1 - b, i + b, False)
                    output(i * 2 + b, b, i, False)
            i = TILES // 2 - 1
            hidden(2 * i, 0, i)
            turn(2 * i + 1, 1, i, False)
            output(2 * i, 0, i, False)
            hidden(2 * i + 1, 1, i)
            output(2 * i + 1, 1, i, False)

        @block.vector
        def _(v):
            n = Count()

            def step(ins):
                ins.then_inc(s_v, 1)
                v.wait_ge(s_v, n.up())

            v.wait_ge(s_edge, 32)
            v.wait_ge(s_const, 14)
            s_, d_, t_ = src_i[0:EP, :], dst_i[0:EP, :], tmp_i[0:EP, :]
            step(v.tensor_scalar(t_, s_, 7, None, ALU.logical_shift_right))
            step(v.tensor_copy(blk16[0:EP, :], t_))
            step(v.tensor_scalar(t_, s_, P - 1, None, ALU.bitwise_and))
            step(v.tensor_scalar(s_, d_, 7, 7, ALU.bitwise_and, ALU.logical_shift_left))
            step(v.tensor_tensor(val2[0:EP, :], t_, s_, ALU.add))
            step(v.tensor_scalar(t_, d_, 3, None, ALU.logical_shift_right))
            v.tensor_scalar(val1[0:EP, :], t_, 1.0, None, ALU.add).then_inc(s_prep, 1)

            def bucket_starts(g, lanes, nb, size, shift):
                v.wait_ge(s_nb[g], 1)
                step(v.tensor_scalar(nbuck_i[0:nb, 0:1], bank[6][0:nb, 0:1], float(size - 1), None, ALU.add))
                step(v.tensor_scalar(nbuck_i[0:nb, 1:2], nbuck_i[0:nb, 0:1], shift, None, ALU.logical_shift_right))
                v.tensor_copy(nbuck[0:nb, 1:2], nbuck_i[0:nb, 1:2]).then_inc(s_nch[g], 1)
                v.wait_ge(s_sc[g], 1)
                step(v.tensor_copy(nbuck[0:nb, 2:3], bank[6][0:nb, 0:1]))
                v.tensor_scalar(diag[0:nb, 0:nb], ident[0:nb, 0:nb], nbuck[0:nb, 2:3], float(size), ALU.mult, ALU.mult)
                m = CH[g] if g < len(CH) else TILES
                v.tensor_scalar(ge[0:nb, 0:m], iota_c[0:nb, 0:m], nbuck[0:nb, 2:3], None, ALU.is_ge).then_inc(s_dg[g], 1)
                v.wait_ge(s_bs[g], 1)
                step(v.tensor_scalar(base[0:lanes, 0:nb], bank[6][0:lanes, 0:nb], -1.0, None, ALU.add))

            def ranks(g):
                c0, C = sum(COLS[:g]), COLS[g]
                b16 = blk16[0:EP, c0:c0 + C]
                with v.Fori(0, NB) as i:
                    for u in range(U):
                        ins = v.tensor_scalar(inb[0:EP, u, 0:C], b16, iota[0:EP, bass.ds(i * U + u, 1)], None, ALU.is_equal, ALU.add,
                                              accum_out=tot[0:EP, bass.ds(i * U + u, 1)])
                    ins.then_inc(s_tot[g], 1)
                    v.wait_ge(s_tot[g], i + 1)
                bucket_starts(g, EP, NT, P, 7)
                step(v.memset(zeros[:, :], 0.0))
                step(v.tensor_scalar(offs[0:1, CH0[g]:CH0[g] + CH[g]], bank[7][0:1, 0:CH[g]], -1.0, float(W), ALU.add, ALU.mult))
                with v.Fori(0, NB) as i:
                    n.enter(i, 3 * U)
                    v.wait_ge(s_v, n.value())
                    for u in range(U):
                        ins = v.tensor_scalar(inb[0:EP, u, 0:C], b16, iota[0:EP, bass.ds(i * U + u, 1)], None, ALU.is_equal)
                        ins.then_inc(s_v, 1)
                        last = n.up()
                    v.wait_ge(s_v, last)
                    for u in range(U + 1):
                        if u < U:
                            if u > 1:
                                v.wait_ge(s_v, n.value())
                            v.tensor_tensor_scan(bank[6 + u % 2][0:EP, 0:C], inb[0:EP, u, 0:C], zeros[0:EP, 0:C],
                                                 base[0:EP, bass.ds(i * U + u, 1)], ALU.add, ALU.add).then_inc(s_v, 1)
                            scanned = n.up()
                        if u > 0:
                            v.wait_ge(s_v, prev if u < U else n.value())
                            v.sem_inc(s_pass)
                            v.copy_predicated(pos[0:EP, 0:C], inb[0:EP, u - 1, 0:C], bank[6 + (u - 1) % 2][0:EP, 0:C]).then_inc(s_v, 1)
                            n.up()
                        prev = scanned
                n.leave(NB)
                v.wait_ge(s_v, n.value())
                ti = tmp_i[0:EP, 0:C]
                step(v.tensor_copy(got_i[0:EP, 0:C], pos[0:EP, 0:C]))
                step(v.tensor_scalar(ti, got_i[0:EP, 0:C], 7, None, ALU.logical_shift_right))
                step(v.tensor_copy(pos_c[0:EP, 0:C], ti))
                step(v.tensor_scalar(ti, got_i[0:EP, 0:C], P - 1, None, ALU.bitwise_and))
                step(v.tensor_copy(pos_q[0:EP, 0:C], ti))

            got_i = got[:, 5, :]
            zeros = ge

            def onehots(g, lanes, c, u, m, q, cc, wait):
                if wait:
                    v.wait_ge(s_pl[g], c - RING[g] + 1)
                v.tensor_scalar(ohq[0:lanes, u % RING[g], :], iota_q[0:lanes, :], q, None, ALU.is_equal).then_inc(s_qc[g], 1)
                v.tensor_scalar(ohc[0:lanes, u % RING[g], 0:m], iota_c[0:lanes, 0:m], cc, None, ALU.is_equal).then_inc(s_qc[g], 1)

            def place_columns(g, lanes, trips, unroll, m, q, cc):
                for u in range(unroll):
                    onehots(g, lanes, u, u, m, q[0:lanes, u:u + 1], cc[0:lanes, u:u + 1], u >= RING[g])
                with v.Fori(1, trips) as i:
                    for u in range(unroll):
                        c = i * unroll + u
                        onehots(g, lanes, c, u, m, q[0:lanes, bass.ds(c, 1)], cc[0:lanes, bass.ds(c, 1)], True)
                v.wait_ge(s_pl[g], trips * unroll + 1)

            def edge_tables(g):
                a, m = CH0[g], CH[g]
                w = [got[:, k, 0:m] for k in range(5)]
                step(v.tensor_scalar(w[0], bank[4][:, 0:m], -1.0, None, ALU.add))
                step(v.tensor_copy(w[1], bank[5][:, 0:m]))
                step(v.tensor_scalar(w[2], w[1], 7, None, ALU.logical_shift_right))
                step(v.tensor_scalar(w[3], w[1], P - 1, None, ALU.bitwise_and))
                step(v.scalar_tensor_tensor(out=w[4], in0=w[0], scalar=8.0, in1=w[2], op0=ALU.mult, op1=ALU.add))
                v.tensor_scalar(rowidx[:, a:a + m], w[4], 0.0, None, ALU.max)
                step(v.tensor_scalar(w[1], w[0], 0.0, -1000.0, ALU.is_lt, ALU.mult))
                v.tensor_tensor(local[:, a:a + m], w[3], w[1], ALU.add).then_inc(s_tab, 1)

            def moments(s_ready):
                with v.Fori(0, NB) as i:
                    n.enter(i, 2)
                    for u in range(U):
                        ins = v.bn_stats(stats[:, u, :], node[:, bass.ds(i * U + u, 1), :].rearrange("p a d -> p (a d)"))
                    step(ins)
                    v.sem_inc(s_pass)
                    for u in range(U):
                        ins = v.bn_aggr(mvt[:, u, :], stats[:, u, :])
                    step(ins)
                    v.tensor_copy(mv[:, bass.ds(i * U, U), :], mvt[:, :, :]).then_inc(s_ready, 1)
                n.leave(NB)

            def normalise(i, u, s_free, first, s_done):
                if not first:
                    v.wait_ge(s_free, (i - 1) * U + u + 1)
                t = bass.ds(i * U + u, 1)
                v.tensor_scalar(xn[:, u, :], node[:, t, :].rearrange("p a d -> p (a d)"), mv[:, t, 0:1].rearrange("p a d -> p (a d)"),
                                rstd[:, t], ALU.subtract, ALU.mult).then_inc(s_done, 1)

            ranks(0)
            v.wait_ge(s_x, 16 * 5)
            moments(s_mv)
            v.wait_ge(s_std, 1)
            step(v.reciprocal(rstd[:, :], std[:, :]))

            def self_add(i, u):
                v.wait_ge(s_mm, i * U + u + 1)
                v.wait_ge(s_bias, i + 1)
                t = node[:, bass.ds(i * U + u, 1), :].rearrange("p a d -> p (a d)")
                v.tensor_tensor(t, t, bank[2 + u % 2][:, 0:D], ALU.add).then_inc(s_add, 1)

            for u in range(U):
                normalise(0, u, s_tr, True, s_xn)
            with v.Fori(0, NB - 1) as i:
                for u in range(U):
                    self_add(i, u)
                    normalise(i + 1, u, s_tr, False, s_xn)
            for u in range(U):
                self_add(NB - 1, u)

            for g in G:
                if g:
                    ranks(g)
                place_columns(g, EP, COLS[g] // PU, PU, CH[g], pos_q, pos_c)
                edge_tables(g)

            def one_hot(c, r, wait):
                if wait:
                    v.wait_ge(s_agg, c - NPS + 1)
                v.tensor_scalar(onehot[:, r % NPS, :], iota[:, :], local[:, bass.ds(c, 1)], None, ALU.is_equal).then_inc(s_oh, 1)

            def sums(i, first):
                _, at = nc.values_load_multi_w_load_instructions(
                    offs[0:1, bass.ds(i * R, R)], engines=[ENG.DVE], min_val=0, max_val=(NT - 1) * W,
                    skip_runtime_bounds_check_because="a count of at most NT - 1 blocks, times W")
                for r in range(R):
                    c = i * R + r
                    one_hot(c + LOOK, r + LOOK, not (first and r + LOOK < NPS))
                    v.wait_ge(s_agg, c + 1)
                    if not (first and r == 0):
                        v.wait_ge(s_sum, c)
                    a = agg[:, bass.ds(at[r], W)]
                    v.tensor_tensor(a, a, bank[r % NPS][:, 0:W], ALU.add).then_inc(s_sum, 1)

            for c in range(LOOK):
                one_hot(c, c, False)
            sums(0, True)
            with v.Fori(1, NCH // R) as i:
                sums(i, False)
            v.wait_ge(s_sum, NCH)

            step(v.tensor_scalar(rcnt[:, :], agg3[:, :, D], 1.0, None, ALU.max))
            step(v.reciprocal(rcnt[:, :], rcnt[:, :]))
            with v.Fori(0, NB) as i:
                n.enter(i, 1)
                for u in range(U):
                    t = bass.ds(i * U + u, 1)
                    h = node[:, t, :].rearrange("p a d -> p (a d)")
                    ins = v.scalar_tensor_tensor(out=h, in0=agg3[:, t, 0:D].rearrange("p a d -> p (a d)"), scalar=rcnt[:, t], in1=h,
                                                 op0=ALU.mult, op1=ALU.add)
                step(ins)
            n.leave(NB)
            moments(s_mv2)
            v.wait_ge(s_std2, 1)
            step(v.reciprocal(rstd[:, :], std[:, :]))

            def scores(i):
                v.wait_ge(s_gate, i * U + U)
                v.tensor_tensor(score[:, bass.ds(i * U, U), :], bank[2][:, 0:U * E].rearrange("p (u e) -> p u e", e=E),
                                gate_b[:, :].rearrange("p (a e) -> p a e", a=1).to_broadcast([P, U, E]), ALU.add).then_inc(s_gadd, 1)

            for u in range(U):
                normalise(0, u, s_tr2, True, s_xn2)
            with v.Fori(1, NB) as i:
                v.wait_ge(s_xst, i * 16)
                for u in range(U):
                    normalise(i, u, s_tr2, False, s_xn2)
                scores(i - 1)
            scores(NB - 1)
            v.wait_ge(s_gadd, NB)

            other = score.rearrange("p t (a f) -> p t a f", a=1).to_broadcast([P, NT, E, E])
            own = score.rearrange("p t (e a) -> p t e a", a=1).to_broadcast([P, NT, E, E])
            v.tensor_tensor(pair[0], other, own, ALU.is_gt)
            step(v.tensor_tensor(pair[1], other, own, ALU.is_equal))
            step(v.tensor_tensor(pair[1], pair[1], earlier[:, :, :].rearrange("p (a e) f -> p a e f", a=1).to_broadcast([P, NT, E, E]), ALU.mult))
            step(v.tensor_tensor(pair[0], pair[0], pair[1], ALU.add))
            step(v.tensor_reduce(rank, pair[0], AX.X, ALU.add))
            for k in range(K):
                step(v.tensor_scalar(sel[k], rank, float(k), None, ALU.is_equal))
                step(v.tensor_tensor(prod, sel[k], score, ALU.mult))
                step(v.tensor_reduce(top[:, k], prod, AX.X, ALU.add))
            v.tensor_tensor(top[:, 1], top[:, 1], top[:, 0], ALU.subtract).then_inc(s_dif, 1)
            step(v.tensor_scalar(vcol[:, 0:1], part[:, :], float(TAIL), None, ALU.is_lt))
            for k in range(K):
                step(v.tensor_scalar(sel[k][:, NT - 1, :], sel[k][:, NT - 1, :], vcol[:, 0:1], None, ALU.mult))
            step(v.tensor_tensor(sel[K], sel[0], sel[1], ALU.add))
            g = len(COLS)
            v.tensor_reduce(tot[:, 0:E], sel[K].rearrange("p t e -> p e t"), AX.X, ALU.add).then_inc(s_tot[g], 1)
            bucket_starts(g, P, E, T, 8)
            step(v.tensor_scalar(texp[0:1, :], bank[7][0:1, 0:TILES], -1.0, None, ALU.add))
            step(v.memset(zeros[:, :], 0.0))
            for e in range(E):
                ins = v.tensor_tensor_scan(cum[:, e, :], sel[K][:, :, e], zeros[:, 0:NT], base[:, e:e + 1], ALU.add, ALU.add)
            step(ins)
            for k in range(K):
                step(v.tensor_tensor(prod, sel[k], cum.rearrange("p e t -> p t e"), ALU.mult))
                step(v.tensor_reduce(tokpos[:, :, k], prod, AX.X, ALU.add))
            step(v.tensor_scalar(vcol[:, 1:2], vcol[:, 0:1], -1.0, -float(4 * SLOTS), ALU.add, ALU.mult))
            step(v.tensor_scalar(tokpos[:, NT - 1, :], tokpos[:, NT - 1, :], vcol[:, 1:2], None, ALU.add))
            flat = tokpos.rearrange("p t k -> p (t k)")
            step(v.tensor_copy(tok_i[0], flat))
            step(v.tensor_scalar(tok_i[1], tok_i[0], 7, None, ALU.logical_shift_right))
            step(v.tensor_copy(tok_c, tok_i[1]))
            step(v.tensor_scalar(tok_i[1], tok_i[0], P - 1, None, ALU.bitwise_and))
            step(v.tensor_copy(tok_q, tok_i[1]))
            tv = tok_v1.rearrange("p (t k) -> p t k", k=K)
            t_col = iota[:, 0:NT].rearrange("p (t a) -> p t a", a=1).to_broadcast([P, NT, K])
            step(v.tensor_scalar(tv, t_col, float(P), part[:, 0:1], ALU.mult, ALU.add))
            step(v.tensor_copy(tok_i[0], tok_v1))
            step(v.tensor_scalar(tok_i[1], tok_i[0], 3, None, ALU.logical_shift_right))
            step(v.tensor_scalar(tok_v1, tok_i[1], 1.0, None, ALU.add))
            step(v.tensor_scalar(tok_i[2], tok_i[0], 7, None, ALU.bitwise_and))
            k_col = iota[:, 0:K].rearrange("p (a k) -> p a k", a=1).to_broadcast([P, NT, K])
            step(v.scalar_tensor_tensor(out=tok_v2.rearrange("p (t k) -> p t k", k=K), in0=k_col, scalar=8.0,
                                        in1=tok_i[2].rearrange("p (t k) -> p t k", k=K), op0=ALU.mult, op1=ALU.add))
            step(v.tensor_scalar(slotid, iota[:, 0:SC], float(P), part[:, 0:1], ALU.mult, ALU.add))
            step(v.tensor_scalar(slotid, slotid, float(K * N + 8), None, ALU.add))
            v.wait_ge(s_exp, 1)
            step(v.tensor_scalar(prob[:, 1], ex, 1.0, None, ALU.add))
            step(v.reciprocal(prob[:, 0], prob[:, 1]))
            step(v.tensor_tensor(prob[:, 1], ex, prob[:, 0], ALU.mult))

            place_columns(g, P, NT * K // RU, RU, SC, tok_q, tok_c)
            w = [got[:, k, 0:SC] for k in range(6)]
            step(v.tensor_scalar(w[0], bank[4][:, 0:SC], -1.0, None, ALU.add))
            step(v.tensor_copy(w[1], bank[5][:, 0:SC]))
            step(v.tensor_scalar(w[2], w[1], 7, None, ALU.bitwise_and))
            step(v.tensor_scalar(w[3], w[1], 3, None, ALU.logical_shift_right))
            step(v.scalar_tensor_tensor(out=w[4], in0=w[0], scalar=8.0, in1=w[2], op0=ALU.mult, op1=ALU.add))
            step(v.tensor_scalar(gidx[:, :], w[4], 0.0, None, ALU.max))
            step(v.scalar_tensor_tensor(out=w[5], in0=w[3], scalar=float(N), in1=w[4], op0=ALU.mult, op1=ALU.add))
            step(v.scalar_tensor_tensor(out=w[1], in0=w[0], scalar=0.0, in1=slotid, op0=ALU.is_lt, op1=ALU.mult))
            v.tensor_tensor(sidx[:, :], w[5], w[1], ALU.add).then_inc(s_route, 1)

            def copy_xT(j, b, first):
                v.wait_ge(s_ft, j + 1)
                if not first:
                    v.wait_ge(s_fh, (j - 1) * HB)
                v.tensor_copy(xgT[:, b].rearrange("p k n -> p (k n)"), bank[0][:, :]).then_inc(s_fx, 1)

            def copy_out(j, b, half, first):
                v.wait_ge(s_fy, j + 1)
                v.wait_ge(s_w2[b], (half + 1) * 32)
                if not first:
                    v.wait_ge(s_sc2[b], half * 16 * TT)
                v.tensor_tensor(ysb[:, b], bank[5 + b][:, :].rearrange("p (n d) -> p n d", d=D),
                                b2b[:, b:b + 1, :].to_broadcast([P, TT, D]), ALU.add).then_inc(s_fo, 1)

            copy_xT(0, 0, True)
            copy_xT(1, 1, True)
            copy_out(0, 0, 0, True)
            copy_xT(2, 0, False)
            copy_out(1, 1, 0, True)
            with v.Fori(1, TILES // 2 - 1) as i:
                copy_xT(i * 2 + 1, 1, False)
                copy_out(i * 2, 0, i, False)
                copy_xT(i * 2 + 2, 0, False)
                copy_out(i * 2 + 1, 1, i, False)
            i = TILES // 2 - 1
            copy_xT(2 * i + 1, 1, False)
            copy_out(2 * i, 0, i, False)
            copy_out(2 * i + 1, 1, i, False)

            loads = 0
            for i in range(NB):
                b = i % 2
                v.wait_ge(s_z[b], 16 * K * (i // 2 + 1) if i < NB - 1 else 16 * (K * (i // 2 + 1) + K))
                for u in range(U):
                    t = i * U + u
                    lanes = P if t < NT - 1 else TAIL
                    h = node[0:lanes, t, :]
                    step(v.scalar_tensor_tensor(out=h, in0=z[0][0:lanes, b, u], scalar=prob[0:lanes, 0, t:t + 1], in1=h, op0=ALU.mult, op1=ALU.add))
                    v.scalar_tensor_tensor(out=h, in0=z[1][0:lanes, b, u], scalar=prob[0:lanes, 1, t:t + 1], in1=h,
                                           op0=ALU.mult, op1=ALU.add).then_inc(s_mix, 1)


def kernel(**inputs):
    import numpy as np
    import concourse.bacc as bacc
    from concourse.bass_utils import run_bass_kernel_spmd as run

    a = {k: np.asarray(v) for k, v in inputs.items()}
    cont = np.ascontiguousarray
    arrays = {
        "x": a["x"], "src": a["src"], "dst": a["dst"],
        "gw1t": cont(a["L0_gnn_W1"].T), "gw2t": cont(a["L0_gnn_W2"].T), "gb1": a["L0_gnn_b1"], "gb2": a["L0_gnn_b2"],
        "wgt": cont(a["L0_ffn_Wg"].T.reshape(DK, P, E).transpose(1, 0, 2)).reshape(P, DK * E),
        "bg": a["L0_ffn_bg"],
        "w1": cont(a["L0_ffn_W1"].reshape(E, H, DK, P).transpose(0, 3, 2, 1)).reshape(E, P, DK * H),
        "b1": cont(a["L0_ffn_b1"].reshape(E, HB, P).transpose(0, 2, 1)),
        "w2": cont(a["L0_ffn_W2"].reshape(E, D, HB, P).transpose(0, 3, 2, 1)).reshape(E, P, HB * D),
        "b2": a["L0_ffn_b2"],
    }
    nc = bacc.Bacc("TRN2", target_bir_lowering=False, num_devices=1)
    args = [nc.dram_tensor(f"in_{k}", v.shape, mybir.dt.from_np(v.dtype), kind="ExternalInput").ap() for k, v in arrays.items()]
    o = nc.dram_tensor("out_0", (N, D), F32, kind="ExternalOutput").ap()
    gnn_moe(nc, *args, o)
    r = run(nc, [{f"in_{k}": cont(v) for k, v in arrays.items()}], core_ids=[0])
    return r.results[0]["out_0"]
```

```python
from contextlib import ExitStack

import concourse.bass as bass
from concourse import mybir

ALU = mybir.AluOpType
ACT = mybir.ActivationFunctionType
AX = mybir.AxisListType
F32 = mybir.dt.float32
F16 = mybir.dt.float16
I32 = mybir.dt.int32
U16 = mybir.dt.uint16
ENG = mybir.EngineType

P = 128
N = 6250
D = 256
DK = D // P
H = 1024
HB = H // P
E = 8
K = 2
EDGES = 100000
NT = -(-N // P)
TAIL = N - (NT - 1) * P
U = 7
NB = NT // U
NP = NT * P
W = D + 1
EPS = 1e-5

EP = 125
EC = EDGES // EP
COLS = [229, 278, 293]


def most_blocks(n, buckets, size):
    return (n + buckets * (size - 1)) // size


R = 16
CH = [-(-most_blocks(EP * c, NT, P) // R) * R for c in COLS]
CH0 = [sum(CH[:g]) for g in range(len(CH))]
NCH = sum(CH)
CMAX, CHMAX = max(COLS), max(CH)
PER = [32, 24, 20]
RB = 13
RT = -(-NT // RB)
LOOPED = [c // p * p for c, p in zip(COLS, PER)]
NPS = 4

T = 256
TT = T // P
TILES = most_blocks(K * N, E, T)
TILES += TILES % 2
SLOTS = TILES * T
SC = SLOTS // P
RING = 4
COLS_E = K * NT
PER_E = 12


class Count:

    def __init__(self):
        self.at = 0
        self.k = 0

    def enter(self, i, per, first=0):
        self.before, self.per = self.at + self.k, per
        self.at, self.k = self.before + (i - first) * per, 0

    def leave(self, trips):
        assert self.k == self.per
        self.at, self.k = self.before + trips * self.per, 0

    def value(self):
        return self.at + self.k

    def up(self):
        self.k += 1
        return self.value()


def gnn_moe(nc, x, src, dst, gw1t, gw2t, gb1, gb2, wgt, bg, w1, b1, w2, b2, out):
    ytab = nc.dram_tensor("ytab", [NP, D], F32, kind="Internal").ap()
    xtab = nc.dram_tensor("xtab", [NP, D], F32, kind="Internal").ap()
    ztab = nc.dram_tensor("ztab", [K * N + SLOTS, D], F32, kind="Internal").ap()

    with ExitStack() as ctx:
        def sb(name, shape, dt=F32):
            return ctx.enter_context(nc.sbuf_tensor(name, shape, dt))

        def sem(name):
            return ctx.enter_context(nc.semaphore(name))

        bank = [ctx.enter_context(nc.psum_tensor(f"bank{i}", [P, 512], F32)) for i in range(8)]

        ident = sb("ident", [P, P])
        ones = sb("ones", [P, P])
        before = sb("before", [P, P])
        iota = sb("iota", [P, P])
        iota_q = sb("iota_q", [P, P], F16)
        iota_c = sb("iota_c", [P, CHMAX], F16)
        zero16 = sb("zero16", [P, P], F16)
        down = sb("down", [P, E])
        part = sb("part", [P, 1])
        node = sb("node", [P, NT, D])
        agg = sb("agg", [P, NT * W])
        agg3 = agg[:, :].rearrange("p (t w) -> p t w", w=W)
        xn = sb("xn", [P, U, D])
        xnT = sb("xnT", [P, U, D])
        yout = sb("yout", [P, U, D])
        total, less_mean, square = (sb(n, [P, NT]) for n in ("total", "less_mean", "square"))
        std = sb("std", [P, NT])
        rstd = sb("rstd", [P, NT])
        eps = sb("eps", [P, 1])
        rcnt = sb("rcnt", [P, NT])
        gw = sb("gw", [P, 2, DK, D])
        gb = sb("gb", [P, 2, D])
        gate_w = sb("gate_w", [P, DK, E])
        gate_b = sb("gate_b", [P, E])
        rowidx = sb("rowidx", [P, NCH], I32)
        minus = sb("minus", [P, NCH])
        offs = sb("offs", [1, NCH], I32)
        stage = sb("stage", [P, R], I32)
        away = sb("away", [P, 2, P])
        onehot = sb("onehot", [P, NPS, P])
        tot = sb("tot", [P, NT])
        nbuck = sb("nbuck", [P, 4])
        nbuck_i = sb("nbuck_i", [P, 2], I32)
        diag = sb("diag", [P, NT])
        base = sb("base", [P, len(COLS), RT * RB])
        ge = sb("ge", [P, CHMAX])
        zeros = sb("zeros", [P, CMAX], F16)
        ohq = sb("ohq", [P, 4, P], F16)
        ohc = sb("ohc", [P, 4, CHMAX], F16)
        val = sb("val", [P, 4, 2, P], F16)
        got = sb("got", [P, 6, CHMAX], I32)
        prob = sb("prob", [P, K, NT])
        gidx = sb("gidx", [P, SC], I32)
        sidx = sb("sidx", [P, SC], I32)
        texp = sb("texp", [1, TILES], I32)
        gstage = sb("gstage", [P, 2, TT], I32)
        sstage = sb("sstage", [P, 2, TT], I32)

        arena = sb("arena", [P, 10752])
        room = [0]

        def take(n, dt=F32):
            a = room[0]
            room[0] += n
            assert room[0] <= 10752
            v = arena[:, a:a + n]
            return v if dt is F32 else v.bitcast(dt)

        rows = take(R * W).rearrange("p (r w) -> p r w", w=W)
        src_i, dst_i = take(EC, I32), take(EC, I32)
        blk16 = take(EC // 2, F16)
        val1, val2 = take(EC), take(EC)
        pos, pos_c, pos_q = take(CMAX), take(CMAX), take(CMAX)
        tmp_i = take(EC, I32)
        inb = take(U * (CMAX + CMAX % 2) // 2, U16).rearrange("p (u c) -> p u c", u=U)

        room[0] = 0
        score = take(NT * E).rearrange("p (t e) -> p t e", e=E)
        sel = [take(NT * E).rearrange("p (t e) -> p t e", e=E) for _ in range(3)]
        cum = take(E * NT).rearrange("p (e t) -> p e t", t=NT)
        prod = take(NT * E).rearrange("p (t e) -> p t e", e=E)
        top = take(K * NT).rearrange("p (k t) -> p k t", k=K)
        ex, chosen = take(NT), take(NT)
        tokpos = take(NT * K).rearrange("p (t k) -> p t k", k=K)
        tok_i = [take(NT * K, I32) for _ in range(3)]
        tok_c, tok_q, tok_v1, tok_v2 = (take(NT * K) for _ in range(4))
        slotid = take(SC)
        vcol = take(2)

        room[0] = 0
        w1b = agg[:, 0:2 * DK * H].rearrange("p (b k h) -> p b k h", b=2, k=DK)
        w2b = agg[:, 2 * DK * H:2 * DK * H + 2 * HB * D].rearrange("p (b k d) -> p b k d", b=2, k=HB)
        hT = take(2 * HB * T // 2 * 1).rearrange("p (k n) -> p k n", k=HB)
        b1b = sb("b1b", [P, 2, HB])
        b2b = sb("b2b", [P, 2, D])
        xg = xn[:, 0:4, :].rearrange("p (b n) d -> p b n d", b=2)
        xgT = xnT[:, 0:4, :].rearrange("p (b k) n -> p b k n", b=2)
        ysb = yout[:, 0:4, :].rearrange("p (b n) d -> p b n d", b=2)
        z = [w1b.rearrange("p b k h -> p b (k h)")[:, :, 0:U * D].rearrange("p b (u d) -> p b u d", d=D),
             w2b.rearrange("p b k d -> p b (k d)")[:, :, 0:U * D].rearrange("p b (u d) -> p b u d", d=D)]

        G = range(len(COLS))
        s_const, s_tail0, s_x, s_edge, s_w = (sem(n) for n in ("consts", "tail_zeroed", "x_in", "edges_in", "weights_in"))
        s_prep = sem("values_ready")
        s_tot = [sem(f"totals{g}") for g in G] + [sem("totals_e")]
        s_nb = [sem(f"counted{g}") for g in G] + [sem("counted_e")]
        s_nch = [sem(f"rounded{g}") for g in G] + [sem("rounded_e")]
        s_sc = [sem(f"starts{g}") for g in G] + [sem("starts_e")]
        s_dg = [sem(f"spread{g}") for g in G] + [sem("spread_e")]
        s_bs = [sem(f"bases{g}") for g in G] + [sem("bases_e")]
        s_qc = [sem(f"onehots{g}") for g in G] + [sem("onehots_e")]
        s_val = [sem(f"scaled{g}") for g in G] + [sem("scaled_e")]
        s_pl = [sem(f"placed{g}") for g in G] + [sem("placed_e")]
        s_tab = sem("tables_ready")
        s_mv, s_std = [sem("summed"), sem("squared")], sem("std")
        s_xn, s_tr, s_xT = sem("normed"), sem("transposed"), sem("xT_ready")
        s_mm, s_bias, s_add, s_y, s_yst = (sem(n) for n in ("linear_done", "biased", "self_added", "y_copied", "y_stored"))
        s_v = sem("vector_steps")
        s_stage, s_away, s_oh, s_agg, s_sum = (sem(n) for n in ("staged", "distances", "onehot_ready", "chunk_multiplied", "chunk_summed"))
        s_row = [sem(f"rows_in{r}") for r in range(R)]
        s_h, s_nm2, s_sq2, s_std2, s_xn2, s_tr2, s_xT2 = (sem(n) for n in ("h_ready", "less_mean2", "squared2", "std2", "normed2", "transposed2", "xT2_ready"))
        s_gate, s_gadd, s_texp = sem("gates_done"), sem("gates_read"), sem("tile_experts")
        s_xst = [sem(f"xtab_stored{u}") for u in range(U)]
        s_dif, s_exp = sem("difference"), sem("exp_done")
        s_route = sem("routed")
        s_rs2 = sem("rstd2")
        s_pass = sem("passed")
        s_gst, s_sst = sem("gather_staged"), sem("scatter_staged")
        s_g2, s_sc2 = [sem(f"tokens_in{b}") for b in (0, 1)], [sem(f"tokens_out{b}") for b in (0, 1)]
        s_w1, s_w2 = [sem(f"w1_in{b}") for b in (0, 1)], [sem(f"w2_in{b}") for b in (0, 1)]
        s_ft, s_fx, s_fh, s_fr, s_fy, s_fo = (sem(n) for n in (
            "ffn_transposed", "ffn_xT", "ffn_hidden", "ffn_relu", "ffn_out", "ffn_biased"))
        s_z, s_mix, s_out = [sem("z_in0"), sem("z_in1")], sem("mixed"), sem("out_stored")

        x_v = x[0:(NT - 1) * P, :].rearrange("(t p) d -> p t d", p=P)
        y_v = ytab.rearrange("(i u p) d -> i p u d", u=U, p=P)
        xt_v = xtab.rearrange("(i u p) d -> i p u d", u=U, p=P)

        def aggregate(eng, trip, begin, ranks=None, placed=lambda g: None):
            for g in G:
                begin(g)
                lo, hi = CH0[g] // R, (CH0[g] + CH[g]) // R
                if g == 0:
                    trip(0, True)
                    lo = 1
                if g + 1 < len(COLS):
                    if ranks:
                        ranks(g + 1, lo, RT)
                    else:
                        with eng.Fori(lo, lo + RT) as i:
                            trip(i, False)
                    lo += RT
                    trip(lo, False, g + 1, 0, True)
                    m = LOOPED[g + 1] // PER[g + 1]
                    with eng.Fori(1, m) as t:
                        trip(lo + t, False, g + 1, t, False)
                    trip(lo + m, False, g + 1, m, False)
                    lo += m + 1
                    placed(g + 1)
                if lo < hi:
                    with eng.Fori(lo, hi) as i:
                        trip(i, False)

        def shared(g, u):
            return g > 0 and u % 2 == 1

        def token_columns(eng, column):
            for u in range(PER_E):
                column(0, u, True)
            with eng.Fori(1, COLS_E // PER_E) as t:
                for u in range(PER_E):
                    column(t, u, False)
            for u in range(COLS_E % PER_E):
                column(COLS_E // PER_E, u, False)

        def columns_of(g, t, r, parts):
            k = min(PER[g], COLS[g] - t * PER[g]) if isinstance(t, int) else PER[g]
            return range(r * k // parts, (r + 1) * k // parts)

        block = ctx.enter_context(nc.Block())

        @block.sync
        def _(sp):
            sp.dma_start(src_i[0:EP, :], src.rearrange("(p c) -> p c", p=EP)).then_inc(s_edge, 16)
            sp.dma_start(dst_i[0:EP, :], dst.rearrange("(p c) -> p c", p=EP)).then_inc(s_edge, 16)
            for a in range(0, NT - 1, 12):
                sp.dma_start(node[:, a:a + 12, :], x_v[:, a:a + 12, :]).then_inc(s_x, 16)
            sp.wait_ge(s_tail0, 1)
            sp.dma_start(node[0:TAIL, NT - 1, :], x[(NT - 1) * P:N, :]).then_inc(s_x, 16)
            sp.dma_start(gw[:, 0], gw1t.rearrange("(k p) n -> p k n", p=P)).then_inc(s_w, 16)
            sp.dma_start(gw[:, 1], gw2t.rearrange("(k p) n -> p k n", p=P)).then_inc(s_w, 16)
            sp.dma_start(gb[:, 0], gb1.rearrange("(a n) -> a n", a=1).to_broadcast([P, D])).then_inc(s_w, 16)
            sp.dma_start(gb[:, 1], gb2.rearrange("(a n) -> a n", a=1).to_broadcast([P, D])).then_inc(s_w, 16)
            sp.dma_start(gate_w[:, :, :], wgt.rearrange("p (k e) -> p k e", e=E)).then_inc(s_w, 16)
            sp.dma_start(gate_b[:, :], bg.rearrange("(a n) -> a n", a=1).to_broadcast([P, E])).then_inc(s_w, 16)
            with sp.Fori(0, NB) as i:
                sp.wait_ge(s_y, i * U + U)
                sp.dma_start(y_v[bass.ds(i, 1)].rearrange("i p u d -> p (i u) d"), yout[:, :, :]).then_inc(s_yst, 16)
            with sp.Fori(0, NB) as i:
                for u in range(U):
                    sp.wait_ge(s_xn2, i * U + u + 1)
                    sp.dma_start(xt_v[bass.ds(i, 1), :, u, :].rearrange("i p d -> p (i d)"), xn[:, u, :]).then_inc(s_xst[u], 16)
            sp.wait_ge(s_texp, 1)

            def weights(j, b, first):
                e = sp.value_load(texp[0:1, bass.ds(j, 1)], min_val=0, max_val=E - 1)
                new = 1
                if not first:
                    new = e != sp.value_load(texp[0:1, bass.ds(j - 2, 1)], min_val=0, max_val=E - 1)
                    sp.wait_ge(s_fh, (j - 1) * HB)
                    sp.wait_ge(s_fr, (j - 1) * HB)
                    sp.sem_inc(s_pass)
                sp.dma_start(w1b[:, b].rearrange("p k h -> p (k h)"),
                             w1[bass.ds(e, 1)].rearrange("e p n -> (e p) n"), cond=new).then_inc(s_w1[b], 16)
                sp.dma_start(b1b[:, b], b1[bass.ds(e, 1)].rearrange("e p n -> (e p) n"), cond=new).then_inc(s_w1[b], 16)
                if not first:
                    sp.wait_ge(s_fo, j - 1)
                    sp.sem_inc(s_pass)
                sp.dma_start(w2b[:, b].rearrange("p k d -> p (k d)"),
                             w2[bass.ds(e, 1)].rearrange("e p n -> (e p) n"), cond=new).then_inc(s_w2[b], 16)
                sp.dma_start(b2b[:, b], b2[bass.ds(e, 1), :].to_broadcast([P, D]), cond=new).then_inc(s_w2[b], 16)

            for j in range(2):
                weights(j, j, True)
            with sp.Fori(1, TILES // 2) as i:
                for b in range(2):
                    weights(i * 2 + b, b, False)
            for b in range(2):
                sp.wait_ge(s_sc2[b], 16 * TT * TILES // 2)
            sp.wait_ge(s_fo, TILES)
            for i in range(NB):
                b = i % 2
                if i >= 2:
                    sp.wait_ge(s_mix, (i - 1) * U)
                for k in range(K):
                    a = k * N + i * U * P
                    full = U if i < NB - 1 else U - 1
                    sp.dma_start(z[k][:, b, 0:full], ztab[a:a + full * P, :].rearrange("(u p) d -> p u d", p=P)).then_inc(s_z[b], 16)
                    if full < U:
                        a += full * P
                        sp.dma_start(z[k][0:TAIL, b, full], ztab[a:a + TAIL, :]).then_inc(s_z[b], 16)
            for i in range(NB):
                sp.wait_ge(s_mix, (i + 1) * U)
                full = U if i < NB - 1 else U - 1
                a = i * U * P
                sp.dma_start(out[a:a + full * P, :].rearrange("(u p) d -> p u d", p=P), node[:, i * U:i * U + full, :]).then_inc(s_out, 16)
                if full < U:
                    a += full * P
                    sp.dma_start(out[a:N, :], node[0:TAIL, NT - 1, :]).then_inc(s_out, 16)
            sp.wait_ge(s_out, 16 * (NB + 1))

        @block.gpsimd
        def _(pool):
            pool.memset(node[:, NT - 1, :], 0.0).then_inc(s_tail0, 1)
            pool.memset(ones[:, :], 1.0).then_inc(s_const, 1)
            pool.iota(iota[:, :], pattern=[[1, P]], base=0, channel_multiplier=0, allow_small_or_imprecise_dtypes=True).then_inc(s_const, 1)
            pool.iota(iota_q[:, :], pattern=[[1, P]], base=0, channel_multiplier=0, allow_small_or_imprecise_dtypes=True).then_inc(s_const, 1)
            pool.iota(iota_c[:, :], pattern=[[1, CHMAX]], base=0, channel_multiplier=0, allow_small_or_imprecise_dtypes=True).then_inc(s_const, 1)
            pool.iota(part[:, :], pattern=[[1, 1]], base=0, channel_multiplier=1, allow_small_or_imprecise_dtypes=True).then_inc(s_const, 1)
            pool.memset(zero16[:, :], 0.0).then_inc(s_const, 1)
            pool.memset(eps[:, :], EPS).then_inc(s_const, 1)
            pool.wait_ge(s_const, 7)
            pool.affine_select(out=ident[:, :], in_=ones[:, :], compare_op=ALU.is_equal, fill=0.0, base=0,
                               pattern=[[-1, P]], channel_multiplier=1).then_inc(s_const, 1)
            pool.affine_select(out=before[:, :], in_=ones[:, :], compare_op=ALU.is_gt, fill=0.0, base=0,
                               pattern=[[1, P]], channel_multiplier=-1).then_inc(s_const, 1)
            pool.iota(down[:, :], pattern=[[-1, E]], base=E, channel_multiplier=0, allow_small_or_imprecise_dtypes=True).then_inc(s_const, 1)
            pool.memset(agg[:, :], 0.0).then_inc(s_const, 1)
            pool.memset(rows[:, :, D:W], 1.0).then_inc(s_const, 1)
            pool.memset(zeros[:, :], 0.0).then_inc(s_const, 1)
            pool.memset(base[:, :, :], 0.0).then_inc(s_const, 1)
            pool.wait_ge(s_w, 16 * 6)
            pool.tensor_tensor(gb[:, 0], gb[:, 0], gb[:, 1], ALU.add).then_inc(s_const, 1)
            pool.wait_ge(s_const, 15)
            with pool.Fori(0, NB) as i:
                pool.wait_ge(s_xn, i * U + U)
                pool.tensor_tensor(node[:, bass.ds(i * U, U), :], node[:, bass.ds(i * U, U), :],
                                   gb[:, 0:1, :].to_broadcast([P, U, D]), ALU.add).then_inc(s_bias, 1)

            pool.wait_ge(s_yst, 16 * NB)

            def gathers(i, first):
                for h in range(2):
                    if not first:
                        pool.wait_ge(s_agg, (i - 1) * R + (h + 1) * (R // 2))
                    pool.tensor_copy(stage[:, h * (R // 2):(h + 1) * (R // 2)],
                                     rowidx[:, bass.ds(i * R + h * (R // 2), R // 2)]).then_inc(s_stage, 1)
                    pool.wait_ge(s_stage, i * 2 + h + 1)
                    pool.sem_inc(s_pass)
                    for r in range(h * (R // 2), (h + 1) * (R // 2)):
                        pool.indirect_dma_start(out=rows[:, r, 0:D], out_offset=None, in_=ytab[:, :],
                                                in_offset=bass.IndirectOffsetOnAxis(ap=stage[:, r:r + 1], axis=0)).then_inc(s_row[r], 16)

            for g in G:
                pool.wait_ge(s_tab, g + 1)
                lo, hi = CH0[g] // R, (CH0[g] + CH[g]) // R
                if g == 0:
                    gathers(0, True)
                    lo = 1
                with pool.Fori(lo, hi) as i:
                    gathers(i, False)

            for u in range(U):
                pool.wait_ge(s_xst[u], 16 * NB)
            pool.wait_ge(s_tr2, NT)

            def fetch(j, b, wait):
                pool.wait_ge(s_gst, j + 1)
                if wait:
                    pool.wait_ge(s_ft, j - 1)
                pool.sem_inc(s_pass)
                for n in range(TT):
                    pool.indirect_dma_start(out=xg[:, b, n, :], out_offset=None, in_=xtab[:, :],
                                            in_offset=bass.IndirectOffsetOnAxis(ap=gstage[:, b, n:n + 1], axis=0)).then_inc(s_g2[b], 16)

            def deliver(j, b):
                pool.wait_ge(s_sst, j + 1)
                pool.wait_ge(s_fo, j + 1)
                pool.sem_inc(s_pass)
                for n in range(TT):
                    pool.indirect_dma_start(out=ztab[:, :], out_offset=bass.IndirectOffsetOnAxis(ap=sstage[:, b, n:n + 1], axis=0),
                                            in_=ysb[:, b, n, :], in_offset=None).then_inc(s_sc2[b], 16)

            fetch(0, 0, False)
            fetch(1, 1, False)
            with pool.Fori(0, TILES // 2 - 1) as i:
                for b in range(2):
                    deliver(i * 2 + b, b)
                    fetch(i * 2 + b + 2, b, True)
            for b in range(2):
                deliver(TILES - 2 + b, b)

        @block.scalar
        def _(act):
            act.wait_ge(s_const, 7)

            def moments(s_pass1, s_pass2, s_done):
                for s_sq in (s_pass1, s_pass2):
                    with act.Fori(0, NB) as i:
                        for u in range(U):
                            t = bass.ds(i * U + u, 1)
                            row = node[:, t, :].rearrange("p a d -> p (a d)")
                            if s_sq is s_pass1:
                                act.activation(xn[:, u, :], row, ACT.Copy, accum_out=total[:, t]).then_inc(s_sq, 1)
                            else:
                                act.activation(xn[:, u, :], row, ACT.Square, bias=less_mean[:, t], accum_out=square[:, t]).then_inc(s_sq, 1)
                        act.wait_ge(s_sq, i * U + U)
                    if s_sq is s_pass1:
                        act.activation(less_mean[:, :], total[:, :], ACT.Copy, scale=-1.0 / D).then_inc(s_pass1, 1)
                        act.wait_ge(s_pass1, NT + 1)
                act.activation(std[:, :], square[:, :], ACT.Sqrt, bias=eps[:, 0:1], scale=1.0 / D).then_inc(s_done, 1)

            act.wait_ge(s_x, 16 * 5)
            moments(s_mv[0], s_mv[1], s_std)

            def scaled(g, c, u, lanes, values, first):
                act.wait_ge(s_qc[g], 2 * c + 1)
                if not (first and u < RING):
                    act.wait_ge(s_pl[g], c - RING + 1)
                k = u % RING
                for which in range(2 if shared(g, u) else 1):
                    ins = act.activation(val[0:lanes, k, which, :], ohq[0:lanes, k, :], ACT.Copy, scale=values[which])
                ins.then_inc(s_val[g], 1)

            def column(g, t, u, first):
                c = t * PER[g] + u
                at = bass.ds(c + sum(COLS[:g]), 1)
                scaled(g, c, u, EP, (val1[0:EP, at], val2[0:EP, at]), first)

            def last_columns(g):
                for c in range(LOOPED[g], COLS[g]):
                    column(g, 0, c, False)

            def linear_out(i, first):
                for u in range(U + 1):
                    if u < U:
                        act.wait_ge(s_tr, i * U + u + 1)
                        act.activation(xnT[:, u, :], bank[u % 2][:, 0:D], ACT.Copy).then_inc(s_xT, 1)
                    if u > 0:
                        act.wait_ge(s_mm, i * U + u)
                        if u == 1 and not first:
                            act.wait_ge(s_yst, i * 16)
                        act.activation(yout[:, u - 1, :], bank[6 + (u - 1) % 2][:, 0:D], ACT.Copy).then_inc(s_y, 1)
                    for k in columns_of(0, i, u, U + 1):
                        column(0, i, k, first)

            linear_out(0, True)
            with act.Fori(1, NB) as i:
                linear_out(i, False)
            last_columns(0)

            def one_hots(i, first, g=None, t=None, first_t=False):
                for r in range(R):
                    c = i * R + r
                    for a in ([0, 1] if r == 0 else [r + 1] if r + 1 < R else []):
                        if not (first and a < 2):
                            act.wait_ge(s_oh, i * R + a - 1)
                        act.activation(away[:, a % 2, :], iota[:, :], ACT.Abs, bias=minus[:, bass.ds(i * R + a, 1)]).then_inc(s_away, 1)
                    act.wait_ge(s_away, c + 1)
                    if not (first and r < NPS):
                        act.wait_ge(s_agg, c - NPS + 1)
                    act.activation(onehot[:, r % NPS, :], away[:, r % 2, :], ACT.Relu, bias=1.0, scale=-1.0).then_inc(s_oh, 1)
                    if g is not None:
                        for u in columns_of(g, t, r, R):
                            column(g, t, u, first_t)

            aggregate(act, one_hots, lambda g: act.wait_ge(s_tab, g + 1))

            def moments_of(i):
                at = bass.ds(i * U, U)
                act.wait_ge(s_h, i * U + U)
                act.activation(less_mean[:, at], total[:, at], ACT.Copy, scale=-1.0 / D).then_inc(s_nm2, 1)
                act.wait_ge(s_nm2, i + 1)
                if not isinstance(i, int):
                    act.wait_ge(s_sq2, i * U)
                for u in range(U):
                    t = bass.ds(i * U + u, 1)
                    act.activation(yout[:, u, :], node[:, t, :].rearrange("p a d -> p (a d)"), ACT.Square,
                                   bias=less_mean[:, t], accum_out=square[:, t]).then_inc(s_sq2, 1)
                act.wait_ge(s_sq2, i * U + U)
                act.activation(std[:, at], square[:, at], ACT.Sqrt, bias=eps[:, 0:1], scale=1.0 / D).then_inc(s_std2, 1)

            def gate_transposes(i):
                for u in range(U):
                    act.wait_ge(s_tr2, i * U + u + 1)
                    act.activation(xnT[:, u, :], bank[u % 2][:, 0:D], ACT.Copy).then_inc(s_xT2, 1)

            moments_of(0)
            with act.Fori(1, NB) as i:
                moments_of(i)
                gate_transposes(i - 1)
            gate_transposes(NB - 1)
            act.wait_ge(s_dif, 1)
            act.activation(ex[:, :], top[:, 1], ACT.Exp).then_inc(s_exp, 1)
            g = len(COLS)

            def token_column(t, u, first):
                one = bass.ds(t * PER_E + u, 1)
                scaled(g, t * PER_E + u, u, P, (tok_v1[:, one], tok_v2[:, one]), first)

            token_columns(act, token_column)

            act.wait_ge(s_route, 1)

            def gstaging(j, b, wait):
                if wait:
                    act.wait_ge(s_ft, j - 1)
                act.activation(gstage[:, b], gidx[:, bass.ds(j * TT, TT)], ACT.Copy).then_inc(s_gst, 1)

            def relu(j, b, first):
                if first:
                    act.activation(sstage[:, b], sidx[:, j * TT:(j + 1) * TT], ACT.Copy).then_inc(s_sst, 1)
                else:
                    act.wait_ge(s_sc2[b], (i_half[0]) * 16 * TT)
                    act.activation(sstage[:, b], sidx[:, bass.ds(j * TT, TT)], ACT.Copy).then_inc(s_sst, 1)
                act.wait_ge(s_w1[b], (i_half[0] + 1) * 32)
                for m in range(HB):
                    act.wait_ge(s_fh, j * HB + m + 1)
                    if not (first and j == 0) and m == 0:
                        act.wait_ge(s_fy, j)
                    act.activation(hT[:, m, :], bank[1 + m % 4][:, 0:T], ACT.Relu, bias=b1b[:, b, m:m + 1]).then_inc(s_fr, 1)

            i_half = [0]
            for j in range(2):
                gstaging(j, j, False)
            for j in range(2):
                relu(j, j, True)
                gstaging(j + 2, j, True)
            with act.Fori(1, TILES // 2 - 1) as i:
                i_half[0] = i
                for b in range(2):
                    relu(i * 2 + b, b, False)
                    gstaging(i * 2 + b + 2, b, True)
            i_half[0] = TILES // 2 - 1
            for b in range(2):
                relu(TILES - 2 + b, b, False)

        @block.tensor
        def _(pe):
            pe.wait_ge(s_const, 15)

            def transposes(i, u, s_in, s_done, s_free):
                pe.wait_ge(s_in, i * U + u + 1)
                back = 1 if u == 0 else 3 if u == 1 else 2
                if not (isinstance(i, int) and u < 2):
                    pe.wait_ge(s_free, i * U + u - back + 1)
                for k in range(DK):
                    mm = pe.transpose(bank[u % 2][:, k * P:(k + 1) * P], xn[:, u, k * P:(k + 1) * P], ident[:, :])
                mm.then_inc(s_done, 1)

            def bucket_sums(g, lanes, nb):
                pe.wait_ge(s_tot[g], NB if g < len(CH) else 1)
                pe.matmul(bank[6][0:nb, 0:1], tot[0:lanes, 0:nb], ones[0:lanes, 0:1], start=True, stop=True).then_inc(s_nb[g], 1)
                pe.wait_ge(s_nch[g], 1)
                pe.matmul(bank[6][0:nb, 0:1], before[0:nb, 0:nb], nbuck[0:nb, 1:2], start=True, stop=True).then_inc(s_sc[g], 1)
                pe.wait_ge(s_dg[g], 1)
                pe.matmul(bank[6][0:lanes, 0:nb], before[0:lanes, 0:lanes], tot[0:lanes, 0:nb], start=True, stop=False)
                pe.matmul(bank[6][0:lanes, 0:nb], ones[0:nb, 0:lanes], diag[0:nb, 0:nb], start=False, stop=True)
                n = CH[g] if g < len(CH) else TILES
                pe.matmul(bank[7][0:1, 0:n], ones[0:nb, 0:1], ge[0:nb, 0:n], start=True, stop=True).then_inc(s_bs[g], 1)

            def place_ends(g, lanes, n, start):
                for v in range(2):
                    mm = pe.matmul(bank[4 + v][:, 0:n], zero16[0:lanes, :], iota_c[0:lanes, 0:n], start=start, stop=not start)
                if not start:
                    mm.then_inc(s_pl[g], 1)

            def place(g, lanes, c, u, n):
                pe.wait_ge(s_qc[g], 2 * c + 2)
                pe.wait_ge(s_val[g], c + 1)
                for v in range(2):
                    mm = pe.matmul(bank[4 + v][:, 0:n], val[0:lanes, u % RING, v, :], ohc[0:lanes, u % RING, 0:n],
                                   start=False, stop=False, skip_group_check=True)
                mm.then_inc(s_pl[g], 1)

            for g in G:
                bucket_sums(g, EP, NT)
            place_ends(0, EP, CH[0], True)

            def linear(i):
                for u in range(U + 1):
                    if u < U:
                        transposes(i, u, s_xn, s_tr, s_xT)
                    if u > 0:
                        m = u - 1
                        pe.wait_ge(s_xT, i * U + m + 1)
                        back = 1 if m == 0 else 3 if m == 1 else 2
                        if not (isinstance(i, int) and m < 2):
                            pe.wait_ge(s_y, i * U + m - back + 1)
                            pe.wait_ge(s_add, i * U + m - back + 1)
                        for half, b in enumerate((2, 6)):
                            for k in range(DK):
                                mm = pe.matmul(bank[b + m % 2][:, 0:D], xnT[:, m, k * P:(k + 1) * P], gw[:, half, k, :],
                                               start=(k == 0), stop=(k == DK - 1))
                        mm.then_inc(s_mm, 1)
                    for k in columns_of(0, i, u, U + 1):
                        place(0, EP, i * PER[0] + k, k, CH[0])

            linear(0)
            with pe.Fori(1, NB) as i:
                linear(i)
            for c in range(LOOPED[0], COLS[0]):
                place(0, EP, c, c, CH[0])
            place_ends(0, EP, CH[0], False)

            def multiply(i, first, g=None, t=None, first_t=False):
                if first_t:
                    pe.wait_ge(s_tab, g)
                    place_ends(g, EP, CH[g], True)
                for r in range(R):
                    n = i * R + r
                    pe.wait_ge(s_row[r], i * 16 + 16)
                    pe.wait_ge(s_oh, n + 1)
                    if not (first and r < NPS):
                        pe.wait_ge(s_sum, n - NPS + 1)
                    pe.matmul(bank[r % NPS][:, 0:W], onehot[:, r % NPS, :], rows[:, r, :], start=True, stop=True).then_inc(s_agg, 1)
                    if g is not None:
                        for u in columns_of(g, t, r, R):
                            place(g, EP, t * PER[g] + u, u, CH[g])

            pe.wait_ge(s_add, NT)
            aggregate(pe, multiply, lambda g: None, placed=lambda g: place_ends(g, EP, CH[g], False))
            pe.wait_ge(s_sum, NCH)
            pe.wait_ge(s_sum, NCH)

            def gates(i):
                for u in range(U + 1):
                    if u < U:
                        transposes(i, u, s_xn2, s_tr2, s_xT2)
                    if u > 0:
                        m = u - 1
                        pe.wait_ge(s_xT2, i * U + m + 1)
                        if m == 0 and not isinstance(i, int):
                            pe.wait_ge(s_gadd, i)
                        for k in range(DK):
                            mm = pe.matmul(bank[2][:, m * E:(m + 1) * E], xnT[:, m, k * P:(k + 1) * P], gate_w[:, k, :],
                                           start=(k == 0), stop=(k == DK - 1))
                        mm.then_inc(s_gate, 1)

            gates(0)
            with pe.Fori(1, NB) as i:
                gates(i)
            bucket_sums(len(COLS), P, E)
            g = len(COLS)
            place_ends(g, P, SC, True)
            token_columns(pe, lambda t, u, first: place(g, P, t * PER_E + u, u, SC))
            place_ends(g, P, SC, False)

            def turn(j, b, half, first):
                pe.wait_ge(s_g2[b], (half + 1) * 16 * TT)
                if not first:
                    pe.wait_ge(s_fx, j)
                for k in range(DK):
                    for n in range(TT):
                        mm = pe.transpose(bank[0][:, k * T + n * P:k * T + (n + 1) * P], xg[:, b, n, k * P:(k + 1) * P], ident[:, :])
                mm.then_inc(s_ft, 1)

            def hidden(j, b, half):
                pe.wait_ge(s_fx, j + 1)
                pe.wait_ge(s_w1[b], (half + 1) * 32)
                for m in range(HB):
                    if not (isinstance(j, int) and j == 0 and m < 4):
                        pe.wait_ge(s_fr, j * HB + m - 3)
                    for k in range(DK):
                        mm = pe.matmul(bank[1 + m % 4][:, 0:T], w1b[:, b, k, m * P:(m + 1) * P], xgT[:, b, k, :],
                                       start=(k == 0), stop=(k == DK - 1))
                    mm.then_inc(s_fh, 1)

            def output(j, b, half, first):
                pe.wait_ge(s_w2[b], (half + 1) * 32)
                if not first:
                    pe.wait_ge(s_fo, j - 1)
                for n in range(TT):
                    for m in range(HB):
                        if n == 0:
                            pe.wait_ge(s_fr, j * HB + m + 1)
                        mm = pe.matmul(bank[5 + b][:, n * D:(n + 1) * D], hT[:, m, n * P:(n + 1) * P], w2b[:, b, m, :],
                                       start=(m == 0), stop=(m == HB - 1))
                mm.then_inc(s_fy, 1)

            pe.wait_ge(s_route, 1)
            turn(0, 0, 0, True)
            hidden(0, 0, 0)
            turn(1, 1, 0, False)
            output(0, 0, 0, True)
            hidden(1, 1, 0)
            turn(2, 0, 1, False)
            output(1, 1, 0, True)
            with pe.Fori(1, TILES // 2 - 1) as i:
                for b in range(2):
                    hidden(i * 2 + b, b, i)
                    turn(i * 2 + b + 1, 1 - b, i + b, False)
                    output(i * 2 + b, b, i, False)
            i = TILES // 2 - 1
            hidden(2 * i, 0, i)
            turn(2 * i + 1, 1, i, False)
            output(2 * i, 0, i, False)
            hidden(2 * i + 1, 1, i)
            output(2 * i + 1, 1, i, False)

        @block.vector
        def _(v):
            n = Count()

            def step(ins):
                ins.then_inc(s_v, 1)
                v.wait_ge(s_v, n.up())

            v.wait_ge(s_edge, 32)
            v.wait_ge(s_const, 15)
            s_, d_, t_ = src_i[0:EP, :], dst_i[0:EP, :], tmp_i[0:EP, :]
            step(v.tensor_scalar(t_, s_, 7, None, ALU.logical_shift_right))
            step(v.tensor_copy(blk16[0:EP, :], t_))
            step(v.tensor_scalar(t_, s_, P - 1, None, ALU.bitwise_and))
            step(v.tensor_scalar(s_, d_, 7, 7, ALU.bitwise_and, ALU.logical_shift_left))
            step(v.tensor_tensor(val2[0:EP, :], t_, s_, ALU.add))
            step(v.tensor_scalar(t_, d_, 3, None, ALU.logical_shift_right))
            v.tensor_scalar(val1[0:EP, :], t_, 1.0, None, ALU.add).then_inc(s_prep, 1)

            def bucket_starts(g, lanes, nb, size, shift):
                v.wait_ge(s_nb[g], 1)
                step(v.tensor_scalar(nbuck_i[0:nb, 0:1], bank[6][0:nb, 0:1], float(size - 1), None, ALU.add))
                step(v.tensor_scalar(nbuck_i[0:nb, 1:2], nbuck_i[0:nb, 0:1], shift, None, ALU.logical_shift_right))
                v.tensor_copy(nbuck[0:nb, 1:2], nbuck_i[0:nb, 1:2]).then_inc(s_nch[g], 1)
                v.wait_ge(s_sc[g], 1)
                step(v.tensor_copy(nbuck[0:nb, 2:3], bank[6][0:nb, 0:1]))
                v.tensor_scalar(diag[0:nb, 0:nb], ident[0:nb, 0:nb], nbuck[0:nb, 2:3], float(size), ALU.mult, ALU.mult)
                m = CH[g] if g < len(CH) else TILES
                v.tensor_scalar(ge[0:nb, 0:m], iota_c[0:nb, 0:m], nbuck[0:nb, 2:3], None, ALU.is_ge).then_inc(s_dg[g], 1)
                v.wait_ge(s_bs[g], 1)
                step(v.tensor_scalar(base[0:lanes, g % len(CH), 0:nb], bank[6][0:lanes, 0:nb], -1.0, None, ALU.add))

            def totals(g):
                c0, C = sum(COLS[:g]), COLS[g]
                with v.Fori(0, NB) as i:
                    for u in range(U):
                        ins = v.tensor_scalar(inb[0:EP, u, 0:C], blk16[0:EP, c0:c0 + C], iota[0:EP, bass.ds(i * U + u, 1)], None,
                                              ALU.is_equal, ALU.add, accum_out=tot[0:EP, bass.ds(i * U + u, 1)])
                    ins.then_inc(s_tot[g], 1)
                    v.wait_ge(s_tot[g], i + 1)
                bucket_starts(g, EP, NT, P, 7)
                step(v.tensor_scalar(offs[0:1, CH0[g]:CH0[g] + CH[g]], bank[7][0:1, 0:CH[g]], -1.0, float(W), ALU.add, ALU.mult))

            def ranks(g, i):
                c0, C = sum(COLS[:g]), COLS[g]
                began = n.value()
                done = {}

                def part_of(r):
                    if r < RB:
                        v.wait_ge(s_v, done["copied", r - 3] if r > 2 else began)
                        v.tensor_scalar(inb[0:EP, r % 3, 0:C], blk16[0:EP, c0:c0 + C], iota[0:EP, bass.ds(i * RB + r, 1)], None,
                                        ALU.is_equal).then_inc(s_v, 1)
                        done["compared", r] = n.up()
                    if 2 <= r < RB + 2:
                        u = r - 2
                        v.wait_ge(s_v, done["scanned", u])
                        v.sem_inc(s_pass)
                        v.copy_predicated(pos[0:EP, 0:C], inb[0:EP, u % 3, 0:C], bank[6 + u % 2][0:EP, 0:C]).then_inc(s_v, 1)
                        done["copied", u] = n.up()
                    if 1 <= r < RB + 1:
                        u = r - 1
                        v.wait_ge(s_v, done["copied", u - 2] if u > 1 else done["compared", u])
                        v.tensor_tensor_scan(bank[6 + u % 2][0:EP, 0:C], inb[0:EP, u % 3, 0:C], zeros[0:EP, 0:C],
                                             base[0:EP, g, bass.ds(i * RB + u, 1)], ALU.add, ALU.add).then_inc(s_v, 1)
                        done["scanned", u] = n.up()

                return part_of

            def positions(g):
                C = COLS[g]
                v.wait_ge(s_v, n.value())
                ti = tmp_i[0:EP, 0:C]
                step(v.tensor_copy(got_i[0:EP, 0:C], pos[0:EP, 0:C]))
                step(v.tensor_scalar(ti, got_i[0:EP, 0:C], 7, None, ALU.logical_shift_right))
                step(v.tensor_copy(pos_c[0:EP, 0:C], ti))
                step(v.tensor_scalar(ti, got_i[0:EP, 0:C], P - 1, None, ALU.bitwise_and))
                step(v.tensor_copy(pos_q[0:EP, 0:C], ti))

            got_i = got[:, 5, :]

            def onehots(g, lanes, c, u, m, q, cc, value, first):
                if not (first and u < RING):
                    v.wait_ge(s_pl[g], c - RING + 1)
                    v.wait_ge(s_val[g], c - RING + 1)
                k = u % RING
                v.tensor_scalar(ohq[0:lanes, k, :], iota_q[0:lanes, :], q, None, ALU.is_equal).then_inc(s_qc[g], 1)
                if not shared(g, u):
                    v.tensor_scalar(val[0:lanes, k, 1, :], iota_q[0:lanes, :], q, value, ALU.is_equal, ALU.mult)
                v.tensor_scalar(ohc[0:lanes, k, 0:m], iota_c[0:lanes, 0:m], cc, None, ALU.is_equal).then_inc(s_qc[g], 1)

            def column(g, t, u, first):
                c = t * PER[g] + u
                one, at = bass.ds(c, 1), bass.ds(c + sum(COLS[:g]), 1)
                onehots(g, EP, c, u, CH[g], pos_q[0:EP, one], pos_c[0:EP, one], val2[0:EP, at], first)

            def last_columns(g):
                for c in range(LOOPED[g], COLS[g]):
                    column(g, 0, c, False)

            def edge_tables(g):
                v.wait_ge(s_pl[g], COLS[g] + 1)
                a, m = CH0[g], CH[g]
                w = [got[:, k, 0:m] for k in range(5)]
                step(v.tensor_scalar(w[0], bank[4][:, 0:m], -1.0, None, ALU.add))
                step(v.tensor_copy(w[1], bank[5][:, 0:m]))
                step(v.tensor_scalar(w[2], w[1], 7, None, ALU.logical_shift_right))
                step(v.tensor_scalar(w[3], w[1], P - 1, None, ALU.bitwise_and))
                step(v.scalar_tensor_tensor(out=w[4], in0=w[0], scalar=8.0, in1=w[2], op0=ALU.mult, op1=ALU.add))
                v.tensor_scalar(rowidx[:, a:a + m], w[4], 0.0, None, ALU.max)
                step(v.tensor_scalar(w[1], w[0], 0.0, 1000.0, ALU.is_lt, ALU.mult))
                v.tensor_tensor(minus[:, a:a + m], w[1], w[3], ALU.subtract).then_inc(s_tab, 1)

            def normalise(i, u, s_free, first, s_done):
                if not first:
                    v.wait_ge(s_free, (i - 1) * U + u + 1)
                t = bass.ds(i * U + u, 1)
                v.tensor_scalar(xn[:, u, :], node[:, t, :].rearrange("p a d -> p (a d)"), less_mean[:, t],
                                rstd[:, t], ALU.add, ALU.mult).then_inc(s_done, 1)

            for g in G:
                totals(g)
            with v.Fori(0, RT) as i:
                n.enter(i, 3 * RB)
                part_of = ranks(0, i)
                for r in range(RB + 2):
                    part_of(r)
            n.leave(RT)
            positions(0)
            v.wait_ge(s_std, 1)
            step(v.reciprocal(rstd[:, :], std[:, :]))

            def self_add(i, u):
                v.wait_ge(s_mm, i * U + u + 1)
                v.wait_ge(s_bias, i + 1)
                t = node[:, bass.ds(i * U + u, 1), :].rearrange("p a d -> p (a d)")
                v.tensor_tensor(t, t, bank[2 + u % 2][:, 0:D], ALU.add).then_inc(s_add, 1)

            for u in range(U):
                normalise(0, u, s_tr, True, s_xn)
            def linear_in(i, first, last):
                for u in range(-1, U):
                    for k in columns_of(0, i, u + 1, U + 1):
                        column(0, i, k, first)
                    if u >= 0:
                        self_add(i, u)
                        if not last:
                            normalise(i + 1, u, s_tr, False, s_xn)

            linear_in(0, True, False)
            with v.Fori(1, NB - 1) as i:
                linear_in(i, False, False)
            linear_in(NB - 1, False, True)
            last_columns(0)
            v.wait_ge(s_y, NT)
            edge_tables(0)

            def sums(i, first, g=None, t=None, first_t=False, beside=None):
                _, at = nc.values_load_multi_w_load_instructions(
                    offs[0:1, bass.ds(i * R, R)], engines=[ENG.DVE], min_val=0, max_val=(NT - 1) * W,
                    skip_runtime_bounds_check_because="a count of at most NT - 1 blocks, times W")

                def columns(r):
                    for u in columns_of(g, t, r, R):
                        column(g, t, u, first_t)

                beside = columns if g is not None else beside or (lambda r: None)
                beside(0)
                for r in range(R):
                    c = i * R + r
                    if r + 1 < R:
                        beside(r + 1)
                    v.wait_ge(s_agg, c + 1)
                    if not (first and r == 0):
                        v.wait_ge(s_sum, c)
                    a = agg[:, bass.ds(at[r], W)]
                    v.tensor_tensor(a, a, bank[r % NPS][:, 0:W], ALU.add).then_inc(s_sum, 1)

            def ranks_beside(g, lo, trips):
                with v.Fori(0, trips) as t:
                    n.enter(t, 3 * RB)
                    sums(t + lo, False, beside=ranks(g, t))
                n.leave(trips)
                positions(g)

            aggregate(v, sums, lambda g: None, ranks_beside, edge_tables)
            v.wait_ge(s_sum, NCH)

            step(v.tensor_scalar(rcnt[:, :], agg3[:, :, D], 1.0, None, ALU.max))
            step(v.reciprocal(rcnt[:, :], rcnt[:, :]))
            def h_rows(i):
                for u in range(U):
                    t = bass.ds(i * U + u, 1)
                    h = node[:, t, :].rearrange("p a d -> p (a d)")
                    v.scalar_tensor_tensor(out=h, in0=agg3[:, t, 0:D].rearrange("p a d -> p (a d)"), scalar=rcnt[:, t], in1=h,
                                           op0=ALU.mult, op1=ALU.add, accum_out=total[:, t]).then_inc(s_h, 1)

            def normed(i, first):
                v.wait_ge(s_std2, i + 1)
                v.reciprocal(rstd[:, bass.ds(i * U, U)], std[:, bass.ds(i * U, U)]).then_inc(s_rs2, 1)
                v.wait_ge(s_rs2, i + 1)
                for u in range(U):
                    if not first:
                        v.wait_ge(s_xst[u], i * 16)
                    normalise(i, u, s_tr2, first, s_xn2)

            def scores(i):
                v.wait_ge(s_gate, i * U + U)
                v.tensor_tensor(score[:, bass.ds(i * U, U), :], bank[2][:, 0:U * E].rearrange("p (u e) -> p u e", e=E),
                                gate_b[:, :].rearrange("p (a e) -> p a e", a=1).to_broadcast([P, U, E]), ALU.add).then_inc(s_gadd, 1)

            h_rows(0)
            h_rows(1)
            normed(0, True)
            with v.Fori(2, NB) as i:
                h_rows(i)
                normed(i - 1, False)
                scores(i - 2)
            normed(NB - 1, False)
            scores(NB - 2)
            scores(NB - 1)
            v.wait_ge(s_gadd, NB)

            def all_experts(a):
                return a.rearrange("p (t a) -> p t a", a=1).to_broadcast([P, NT, E])

            later = down[:, :].rearrange("p (a e) -> p a e", a=1).to_broadcast([P, NT, E])
            for k in range(K):
                step(v.tensor_reduce(top[:, k], score, AX.X, ALU.max))
                step(v.tensor_tensor(prod, score, all_experts(top[:, k]), ALU.is_equal))
                step(v.tensor_tensor(prod, prod, later, ALU.mult))
                step(v.tensor_reduce(chosen, prod, AX.X, ALU.max))
                step(v.tensor_tensor(sel[k], later, all_experts(chosen), ALU.is_equal))
                if k < K - 1:
                    step(v.scalar_tensor_tensor(out=score, in0=sel[k], scalar=-3e38, in1=score, op0=ALU.mult, op1=ALU.add))
            v.tensor_tensor(top[:, 1], top[:, 1], top[:, 0], ALU.subtract).then_inc(s_dif, 1)
            step(v.tensor_scalar(vcol[:, 0:1], part[:, :], float(TAIL), None, ALU.is_lt))
            for k in range(K):
                step(v.tensor_scalar(sel[k][:, NT - 1, :], sel[k][:, NT - 1, :], vcol[:, 0:1], None, ALU.mult))
            step(v.tensor_tensor(sel[K], sel[0], sel[1], ALU.add))
            g = len(COLS)
            v.tensor_reduce(tot[:, 0:E], sel[K].rearrange("p t e -> p e t"), AX.X, ALU.add).then_inc(s_tot[g], 1)
            bucket_starts(g, P, E, T, 8)
            v.tensor_scalar(texp[0:1, :], bank[7][0:1, 0:TILES], -1.0, None, ALU.add).then_inc(s_texp, 1)
            for e in range(E):
                ins = v.tensor_tensor_scan(cum[:, e, :], sel[K][:, :, e], zeros[:, 0:NT], base[:, 0, e:e + 1], ALU.add, ALU.add)
            step(ins)
            for k in range(K):
                step(v.tensor_tensor(prod, sel[k], cum.rearrange("p e t -> p t e"), ALU.mult))
                step(v.tensor_reduce(tokpos[:, :, k], prod, AX.X, ALU.add))
            step(v.tensor_scalar(vcol[:, 1:2], vcol[:, 0:1], -1.0, -float(4 * SLOTS), ALU.add, ALU.mult))
            step(v.tensor_scalar(tokpos[:, NT - 1, :], tokpos[:, NT - 1, :], vcol[:, 1:2], None, ALU.add))
            flat = tokpos.rearrange("p t k -> p (t k)")
            step(v.tensor_copy(tok_i[0], flat))
            step(v.tensor_scalar(tok_i[1], tok_i[0], 7, None, ALU.logical_shift_right))
            step(v.tensor_copy(tok_c, tok_i[1]))
            step(v.tensor_scalar(tok_i[1], tok_i[0], P - 1, None, ALU.bitwise_and))
            step(v.tensor_copy(tok_q, tok_i[1]))
            tv = tok_v1.rearrange("p (t k) -> p t k", k=K)
            t_col = iota[:, 0:NT].rearrange("p (t a) -> p t a", a=1).to_broadcast([P, NT, K])
            step(v.tensor_scalar(tv, t_col, float(P), part[:, 0:1], ALU.mult, ALU.add))
            step(v.tensor_copy(tok_i[0], tok_v1))
            step(v.tensor_scalar(tok_i[1], tok_i[0], 3, None, ALU.logical_shift_right))
            step(v.tensor_scalar(tok_v1, tok_i[1], 1.0, None, ALU.add))
            step(v.tensor_scalar(tok_i[2], tok_i[0], 7, None, ALU.bitwise_and))
            k_col = iota[:, 0:K].rearrange("p (a k) -> p a k", a=1).to_broadcast([P, NT, K])
            step(v.scalar_tensor_tensor(out=tok_v2.rearrange("p (t k) -> p t k", k=K), in0=k_col, scalar=8.0,
                                        in1=tok_i[2].rearrange("p (t k) -> p t k", k=K), op0=ALU.mult, op1=ALU.add))
            step(v.tensor_scalar(slotid, iota[:, 0:SC], float(P), part[:, 0:1], ALU.mult, ALU.add))
            step(v.tensor_scalar(slotid, slotid, float(K * N + 8), None, ALU.add))
            v.wait_ge(s_exp, 1)
            step(v.tensor_scalar(prob[:, 1], ex, 1.0, None, ALU.add))
            step(v.reciprocal(prob[:, 0], prob[:, 1]))
            step(v.tensor_tensor(prob[:, 1], ex, prob[:, 0], ALU.mult))

            def token_column(t, u, first):
                c = t * PER_E + u
                one = bass.ds(c, 1)
                onehots(g, P, c, u, SC, tok_q[:, one], tok_c[:, one], tok_v2[:, one], first)

            token_columns(v, token_column)
            v.wait_ge(s_pl[g], NT * K + 1)
            w = [got[:, k, 0:SC] for k in range(6)]
            step(v.tensor_scalar(w[0], bank[4][:, 0:SC], -1.0, None, ALU.add))
            step(v.tensor_copy(w[1], bank[5][:, 0:SC]))
            step(v.tensor_scalar(w[2], w[1], 7, None, ALU.bitwise_and))
            step(v.tensor_scalar(w[3], w[1], 3, None, ALU.logical_shift_right))
            step(v.scalar_tensor_tensor(out=w[4], in0=w[0], scalar=8.0, in1=w[2], op0=ALU.mult, op1=ALU.add))
            step(v.tensor_scalar(gidx[:, :], w[4], 0.0, None, ALU.max))
            step(v.scalar_tensor_tensor(out=w[5], in0=w[3], scalar=float(N), in1=w[4], op0=ALU.mult, op1=ALU.add))
            step(v.scalar_tensor_tensor(out=w[1], in0=w[0], scalar=0.0, in1=slotid, op0=ALU.is_lt, op1=ALU.mult))
            v.tensor_tensor(sidx[:, :], w[5], w[1], ALU.add).then_inc(s_route, 1)

            def copy_xT(j, b, first):
                v.wait_ge(s_ft, j + 1)
                if not first:
                    v.wait_ge(s_fh, (j - 1) * HB)
                v.tensor_copy(xgT[:, b].rearrange("p k n -> p (k n)"), bank[0][:, :]).then_inc(s_fx, 1)

            def copy_out(j, b, half, first):
                v.wait_ge(s_fy, j + 1)
                v.wait_ge(s_w2[b], (half + 1) * 32)
                if not first:
                    v.wait_ge(s_sc2[b], half * 16 * TT)
                v.tensor_tensor(ysb[:, b], bank[5 + b][:, :].rearrange("p (n d) -> p n d", d=D),
                                b2b[:, b:b + 1, :].to_broadcast([P, TT, D]), ALU.add).then_inc(s_fo, 1)

            copy_xT(0, 0, True)
            copy_xT(1, 1, True)
            copy_out(0, 0, 0, True)
            copy_xT(2, 0, False)
            copy_out(1, 1, 0, True)
            with v.Fori(1, TILES // 2 - 1) as i:
                copy_xT(i * 2 + 1, 1, False)
                copy_out(i * 2, 0, i, False)
                copy_xT(i * 2 + 2, 0, False)
                copy_out(i * 2 + 1, 1, i, False)
            i = TILES // 2 - 1
            copy_xT(2 * i + 1, 1, False)
            copy_out(2 * i, 0, i, False)
            copy_out(2 * i + 1, 1, i, False)

            loads = 0
            for i in range(NB):
                b = i % 2
                v.wait_ge(s_z[b], 16 * K * (i // 2 + 1) if i < NB - 1 else 16 * (K * (i // 2 + 1) + K))
                for u in range(U):
                    t = i * U + u
                    lanes = P if t < NT - 1 else TAIL
                    h = node[0:lanes, t, :]
                    step(v.scalar_tensor_tensor(out=h, in0=z[0][0:lanes, b, u], scalar=prob[0:lanes, 0, t:t + 1], in1=h, op0=ALU.mult, op1=ALU.add))
                    v.scalar_tensor_tensor(out=h, in0=z[1][0:lanes, b, u], scalar=prob[0:lanes, 1, t:t + 1], in1=h,
                                           op0=ALU.mult, op1=ALU.add).then_inc(s_mix, 1)


def kernel(**inputs):
    import numpy as np
    import concourse.bacc as bacc
    from concourse.bass_utils import run_bass_kernel_spmd as run

    a = {k: np.asarray(v) for k, v in inputs.items()}
    cont = np.ascontiguousarray
    arrays = {
        "x": a["x"], "src": a["src"], "dst": a["dst"],
        "gw1t": cont(a["L0_gnn_W1"].T), "gw2t": cont(a["L0_gnn_W2"].T), "gb1": a["L0_gnn_b1"], "gb2": a["L0_gnn_b2"],
        "wgt": cont(a["L0_ffn_Wg"].T.reshape(DK, P, E).transpose(1, 0, 2)).reshape(P, DK * E),
        "bg": a["L0_ffn_bg"],
        "w1": cont(a["L0_ffn_W1"].reshape(E, H, DK, P).transpose(0, 3, 2, 1)).reshape(E, P, DK * H),
        "b1": cont(a["L0_ffn_b1"].reshape(E, HB, P).transpose(0, 2, 1)),
        "w2": cont(a["L0_ffn_W2"].reshape(E, D, HB, P).transpose(0, 3, 2, 1)).reshape(E, P, HB * D),
        "b2": a["L0_ffn_b2"],
    }
    nc = bacc.Bacc("TRN2", target_bir_lowering=False, num_devices=1)
    args = [nc.dram_tensor(f"in_{k}", v.shape, mybir.dt.from_np(v.dtype), kind="ExternalInput").ap() for k, v in arrays.items()]
    o = nc.dram_tensor("out_0", (N, D), F32, kind="ExternalOutput").ap()
    gnn_moe(nc, *args, o)
    r = run(nc, [{f"in_{k}": cont(v) for k, v in arrays.items()}], core_ids=[0])
    return r.results[0]["out_0"]
```
